# Optimizing a Trainium2 kernel written in Bass

```python
import numpy as np
import jax
import jax.numpy as jnp

def _softmax(x, axis=-1):
    return jax.nn.softmax(x, axis=axis)

def _gelu(x):
    return jax.nn.gelu(x, approximate=True)

def _silu(x):
    return jax.nn.silu(x)

def _sigmoid(x):
    return jax.nn.sigmoid(x)

def _layernorm(x, axis=-1, eps=1e-05):
    m = jnp.mean(x, axis=axis, keepdims=True)
    v = jnp.var(x, axis=axis, keepdims=True)
    return (x - m) / jnp.sqrt(v + eps)

def _scatter_add(tgt, idx, src, axis=0):
    return tgt.at[idx].add(src)

def _segment_sum(src, seg, n):
    return jax.ops.segment_sum(src, seg, n)
kernel_name = 'mk_adaln_ffn_d2_seqx_r8_296993'

def setup_inputs(seed: int=0):
    np.random.seed(seed)
    _w = jnp.asarray

    def _rec_inputs():
        import jax
        import jax.numpy as jnp
        _rk = jax.random.key(seed)
        x = -0.000125 + 0.9999 * jax.random.normal(jax.random.fold_in(_rk, 1), (32, 32, 512), jnp.float32)
        _lenS = 32 - jax.random.randint(jax.random.fold_in(_rk, 7), (32,), 0, max(1, 32 // 4) + 1, jnp.int32)
        _lenS2 = 32 - jax.random.randint(jax.random.fold_in(_rk, 8), (32,), 0, max(1, 32 // 4) + 1, jnp.int32)
        cond_128 = 0.0061147 + 1.02565 * jax.random.normal(jax.random.fold_in(_rk, 11), (32, 128), jnp.float32)
        fside_S_0 = -0.022604 + 0.987366 * jax.random.normal(jax.random.fold_in(_rk, 12), (32,), jnp.float32)
        return (x, cond_128, fside_S_0)
    x, cond_128, fside_S_0 = _rec_inputs()

    def _L0_cond_setup():
        import jax, jax.numpy as jnp
        import numpy as np
        from jax import lax
        N, C_IN, L = (32, 32, 512)
        C_OUT, K, GROUPS = (32, 9, 4)
        C_DIM, PAD, STRIDE = (128, 4, 1)
        key = jax.random.key(seed)
        k1, k2, k3, k4, k5 = jax.random.split(key, 5)
        x = jax.random.normal(k1, (N, C_IN, L), dtype=jnp.float32)
        c = jax.random.normal(k2, (N, C_DIM), dtype=jnp.float32)
        weight = jax.random.normal(k3, (C_OUT, C_IN // GROUPS, K), dtype=jnp.float32)
        c_weight = jax.random.normal(k4, (C_OUT, C_DIM), dtype=jnp.float32)
        bias = jax.random.normal(k5, (C_OUT,), dtype=jnp.float32)
        return {'x': x, 'c': c, 'weight': weight, 'c_weight': c_weight, 'bias': bias}
    _L0_cond_all = _L0_cond_setup()
    _L0_cond_in = {k: v for k, v in _L0_cond_all.items() if k in ('weight', 'c_weight')}
    del _L0_cond_all

    def _L0_ffn_setup():
        import jax, jax.numpy as jnp
        import numpy as np
        _TRIPLES = [(1, 2, 3), (1, 4, 5), (1, 7, 6), (2, 4, 6), (2, 5, 7), (3, 4, 7), (3, 6, 5)]

        def _oct_struct():
            S = np.zeros((8, 8, 8), np.float32)
            S[0, 0, 0] = 1.0
            for i in range(1, 8):
                S[0, i, i] = 1.0
                S[i, 0, i] = 1.0
                S[i, i, 0] = -1.0
            for a, b, c in _TRIPLES:
                for x, y, z in ((a, b, c), (b, c, a), (c, a, b)):
                    S[x, y, z] = 1.0
                    S[y, x, z] = -1.0
            return jnp.asarray(S)
        S_OCT = _oct_struct()
        N_EMBD = 512
        HIDDEN = 1366

        def ternary_dequant(W):
            scale = jnp.mean(jnp.abs(W))
            Wq = scale * jnp.clip(jnp.round(W / scale), -1.0, 1.0)
            return W + jax.lax.stop_gradient(Wq - W)

        def oct_ternary_linear(xp, W):
            Wq = ternary_dequant(W)
            M = jnp.einsum('jik,jod->koid', S_OCT, Wq)
            return jnp.einsum('...id,koid->...ko', xp, M)
        key = jax.random.key(seed)
        k1, k2, k3, k4 = jax.random.split(key, 4)
        B, T = (2, 256)
        d8, h8 = (N_EMBD // 8, HIDDEN // 8)
        std_in = 1.0 / np.sqrt(N_EMBD)
        std_h = 1.0 / np.sqrt(HIDDEN)
        return {'x': jax.random.normal(k1, (B, T, N_EMBD), jnp.float32), 'w_gate': jax.random.normal(k2, (8, h8, d8), jnp.float32) * std_in, 'w_up': jax.random.normal(k3, (8, h8, d8), jnp.float32) * std_in, 'w_down': jax.random.normal(k4, (8, d8, h8), jnp.float32) * std_h}
    _L0_ffn_all = _L0_ffn_setup()
    _L0_ffn_in = {k: v for k, v in _L0_ffn_all.items() if k in ('w_gate', 'w_up', 'w_down')}
    del _L0_ffn_all

    def _L1_cond_setup():
        import jax, jax.numpy as jnp
        import numpy as np
        K = 8
        T = 1.0
        D_EMBD = 128
        IN_C = 32
        OUT_C = 32
        BS = 32
        H = 512
        HID = 128
        key = jax.random.key(seed)
        ks = jax.random.split(key, 10)
        s = lambda fan_in: 1.0 / np.sqrt(fan_in)
        return {'x': jax.random.normal(ks[0], (BS, IN_C, H), dtype=jnp.float32), 'embedding': jax.random.normal(ks[1], (BS, D_EMBD), dtype=jnp.float32), 'W0': jax.random.normal(ks[2], (D_EMBD, HID), dtype=jnp.float32) * s(D_EMBD), 'b0': jnp.zeros((HID,), dtype=jnp.float32), 'W1': jax.random.normal(ks[3], (HID, HID), dtype=jnp.float32) * s(HID), 'b1': jnp.zeros((HID,), dtype=jnp.float32), 'W2': jax.random.normal(ks[4], (HID, K), dtype=jnp.float32) * s(HID), 'b2': jnp.zeros((K,), dtype=jnp.float32), 'weight': jax.random.normal(ks[5], (K, OUT_C, IN_C, 1), dtype=jnp.float32) * s(IN_C), 'bias_k': jax.random.normal(ks[6], (K, OUT_C), dtype=jnp.float32) * 0.1}
    _L1_cond_all = _L1_cond_setup()
    _L1_cond_in = {k: v for k, v in _L1_cond_all.items() if k in ('W0', 'b0', 'W1', 'b1', 'W2', 'b2', 'weight', 'bias_k')}
    del _L1_cond_all

    def _L1_ffn_setup():
        import jax, jax.numpy as jnp
        import numpy as np
        NUM_EXPERTS = 32
        D_MODEL = 512
        TOP_K = 2
        key = jax.random.key(seed)
        k1, k2, k3, k4 = jax.random.split(key, 4)
        x = jax.random.normal(k1, (2, 256, D_MODEL), dtype=jnp.float32)
        gate_w = jax.random.normal(k2, (NUM_EXPERTS, D_MODEL), dtype=jnp.float32) * 0.02
        expert_w = jax.random.normal(k3, (NUM_EXPERTS, D_MODEL, D_MODEL), dtype=jnp.float32) * 0.02
        expert_b = jax.random.normal(k4, (NUM_EXPERTS, D_MODEL), dtype=jnp.float32) * 0.02
        return {'x': x, 'gate_w': gate_w, 'expert_w': expert_w, 'expert_b': expert_b}
    _L1_ffn_all = _L1_ffn_setup()
    _L1_ffn_in = {k: v for k, v in _L1_ffn_all.items() if k in ('gate_w', 'expert_w', 'expert_b')}
    del _L1_ffn_all
    return {'x': x, 'cond_128': cond_128, 'fside_S_0': fside_S_0, 'L0_cond_weight': _L0_cond_in['weight'], 'L0_cond_c_weight': _L0_cond_in['c_weight'], 'L0_ffn_w_gate': _L0_ffn_in['w_gate'], 'L0_ffn_w_up': _L0_ffn_in['w_up'], 'L0_ffn_w_down': _L0_ffn_in['w_down'], 'L1_cond_W0': _L1_cond_in['W0'], 'L1_cond_b0': _L1_cond_in['b0'], 'L1_cond_W1': _L1_cond_in['W1'], 'L1_cond_b1': _L1_cond_in['b1'], 'L1_cond_W2': _L1_cond_in['W2'], 'L1_cond_b2': _L1_cond_in['b2'], 'L1_cond_weight': _L1_cond_in['weight'], 'L1_cond_bias_k': _L1_cond_in['bias_k'], 'L1_ffn_gate_w': _L1_ffn_in['gate_w'], 'L1_ffn_expert_w': _L1_ffn_in['expert_w'], 'L1_ffn_expert_b': _L1_ffn_in['expert_b']}

def reference(x, cond_128, fside_S_0, L0_cond_weight, L0_cond_c_weight, L0_ffn_w_gate, L0_ffn_w_up, L0_ffn_w_down, L1_cond_W0, L1_cond_b0, L1_cond_W1, L1_cond_b1, L1_cond_W2, L1_cond_b2, L1_cond_weight, L1_cond_bias_k, L1_ffn_gate_w, L1_ffn_expert_w, L1_ffn_expert_b):
    import jax
    import jax.numpy as jnp

    def _L0_cond_ref(x, c, weight, c_weight, bias):
        import jax, jax.numpy as jnp
        import numpy as np
        from jax import lax
        N, C_IN, L = (32, 32, 512)
        C_OUT, K, GROUPS = (32, 9, 4)
        C_DIM, PAD, STRIDE = (128, 4, 1)
        out = lax.conv_general_dilated(x, weight, window_strides=(STRIDE,), padding=[(PAD, PAD)], dimension_numbers=('NCH', 'OIH', 'NCH'), feature_group_count=GROUPS)
        ctx = jnp.einsum('nd,od->no', c, c_weight)
        out = out + ctx[:, :, None] + bias[None, :, None]
        return out

    def _L0_ffn_ref(x, w_gate, w_up, w_down):
        import jax, jax.numpy as jnp
        import numpy as np
        _TRIPLES = [(1, 2, 3), (1, 4, 5), (1, 7, 6), (2, 4, 6), (2, 5, 7), (3, 4, 7), (3, 6, 5)]

        def _oct_struct():
            S = np.zeros((8, 8, 8), np.float32)
            S[0, 0, 0] = 1.0
            for i in range(1, 8):
                S[0, i, i] = 1.0
                S[i, 0, i] = 1.0
                S[i, i, 0] = -1.0
            for a, b, c in _TRIPLES:
                for x, y, z in ((a, b, c), (b, c, a), (c, a, b)):
                    S[x, y, z] = 1.0
                    S[y, x, z] = -1.0
            return jnp.asarray(S)
        S_OCT = _oct_struct()
        N_EMBD = 512
        HIDDEN = 1366

        def ternary_dequant(W):
            scale = jnp.mean(jnp.abs(W))
            Wq = scale * jnp.clip(jnp.round(W / scale), -1.0, 1.0)
            return W + jax.lax.stop_gradient(Wq - W)

        def oct_ternary_linear(xp, W):
            Wq = ternary_dequant(W)
            M = jnp.einsum('jik,jod->koid', S_OCT, Wq)
            return jnp.einsum('...id,koid->...ko', xp, M)
        B, T, D = x.shape
        xp = x.reshape(B, T, 8, D // 8)
        gate = oct_ternary_linear(xp, w_gate).reshape(B, T, -1)
        up = oct_ternary_linear(xp, w_up).reshape(B, T, -1)
        h = jax.nn.silu(gate) * up
        hp = h.reshape(B, T, 8, h.shape[-1] // 8)
        out = oct_ternary_linear(hp, w_down).reshape(B, T, D)
        return out

    def _L1_cond_ref(x, embedding, W0, b0, W1, b1, W2, b2, weight, bias_k):
        import jax, jax.numpy as jnp
        import numpy as np
        K = 8
        T = 1.0
        D_EMBD = 128
        IN_C = 32
        OUT_C = 32
        BS = 32
        H = 512
        HID = 128
        h = jax.nn.gelu(embedding @ W0 + b0, approximate=False)
        h = jax.nn.gelu(h @ W1 + b1, approximate=False)
        att = jax.nn.softmax((h @ W2 + b2) / T, axis=-1)
        agg_w = jnp.einsum('bk,koi->boi', att, weight[..., 0])
        agg_b = att @ bias_k
        out = jnp.einsum('boi,bih->boh', agg_w, x) + agg_b[:, :, None]
        return out

    def _L1_ffn_ref(x, gate_w, expert_w, expert_b):
        import jax, jax.numpy as jnp
        import numpy as np
        NUM_EXPERTS = 32
        D_MODEL = 512
        TOP_K = 2
        B, S, D = x.shape
        T = B * S
        xf = x.reshape(T, D)
        logits = xf @ gate_w.T
        w, idx = jax.lax.top_k(logits, TOP_K)
        w = jax.nn.softmax(w, axis=-1)
        combine = jnp.zeros((T, NUM_EXPERTS), dtype=x.dtype).at[jnp.arange(T)[:, None], idx].add(w)

        def body(acc, params):
            W, b, c = params
            return (acc + c[:, None] * (xf @ W.T + b), None)
        out, _ = jax.lax.scan(body, jnp.zeros_like(xf), (expert_w, expert_b, combine.T))
        return out.reshape(B, S, D)
    x = x + _L0_ffn_ref(_L0_cond_ref(x, cond_128, L0_cond_weight, L0_cond_c_weight, fside_S_0), L0_ffn_w_gate, L0_ffn_w_up, L0_ffn_w_down)
    x = x + _L1_ffn_ref(_L1_cond_ref(x, cond_128, L1_cond_W0, L1_cond_b0, L1_cond_W1, L1_cond_b1, L1_cond_W2, L1_cond_b2, L1_cond_weight, L1_cond_bias_k), L1_ffn_gate_w, L1_ffn_expert_w, L1_ffn_expert_b)
    return x

_drawn_inputs = setup_inputs


def setup_inputs(seed=0):
    import zlib

    import numpy as np

    out = dict(_drawn_inputs(seed))
    spreads = {'L1_cond_b0': (0.0, 0.496), 'L1_cond_b1': (0.0, 0.349), 'L1_cond_b2': (0.0, 0.295)}
    factors = {'L1_cond_bias_k': 51.375, 'L1_ffn_expert_b': 181.53}
    for name, (base, spread) in spreads.items():
        noise = np.random.default_rng([zlib.crc32(name.encode()), seed]).standard_normal(out[name].shape)
        drawn = base * np.exp(spread * noise) if base else spread * noise
        out[name] = jnp.asarray(drawn.astype(out[name].dtype))
    for name, factor in factors.items():
        out[name] = (out[name] * factor).astype(out[name].dtype)
    return out
```

```python
import concourse.bass as bass
from concourse import mybir
from contextlib import ExitStack

F32 = mybir.dt.float32
F32R = mybir.dt.float32r
BF16 = mybir.dt.bfloat16
I32 = mybir.dt.int32
U32 = mybir.dt.uint32
ALU = mybir.AluOpType
ACT = mybir.ActivationFunctionType
AX = mybir.AxisListType

P = 128
NB, CH, D = 32, 32, 512
TOK = NB * CH
NT = TOK // P
NPT = P // CH
R = D // P
TAPS = 9
QW = P + 2
OCT = 8
IN8, HID8, OUT8 = D // OCT, 170, D // OCT
OB = P // OCT
HC = -(-HID8 // OB)
HALF = TOK // 2
TPH = NT // 2
BW = HC * IN8
KC = 8
E = 32
DC = D // P
U = 8
EARLY = 3
LAG = 3
XU = 2
G0 = E // U
CHUNKS = TOK // P
XMAX = 16
PADROW = 1 << 20

C_ID, C_IO, C_MK, C_TRI, C_THR, C_ONE = 0, 128, 160, 164, 196, 204
CF_W = C_ONE + P
B_UP, B_ONE = 0, P
CB_W = 2 * P


def build_adaln_ffn(nc, a):
    ctx = ExitStack()
    with ctx:
        def dram(name, shape, dt):
            return nc.dram_tensor(name, shape, dt, kind="Internal").ap()

        y_tab = dram("y_tab", (TOK, D), F32)
        slots = dram("slots", ((CHUNKS + 1) * P * E, 4), I32)
        picked = dram("picked", (2 * TOK, D), F32)
        slots_v = slots.rearrange("(c p e) w -> c p e w", p=P, e=E)

        cur = [-(-nc.sbuf_base // 32) * 32]

        def region(size):
            at = cur[0]
            cur[0] += -(-size // 32) * 32
            assert cur[0] <= nc.sbuf_usable_end, (cur[0], nc.sbuf_usable_end)
            return at

        def put(name, shape, dt, at):
            return nc.alloc_sbuf_tensor_at(name, shape, dt, offset=at)

        def own(name, shape, dt):
            n = 4 if dt != BF16 else 2
            for s in shape[1:]:
                n *= s
            return put(name, shape, dt, region(n))

        class Cursor:

            def __init__(self, at, size):
                self.at, self.end = at, at + size

            def put(self, name, shape, dt):
                n = 4 if dt != BF16 else 2
                for s in shape[1:]:
                    n *= s
                t = put(name, shape, dt, self.at)
                self.at += -(-n // 32) * 32
                assert self.at <= self.end, name
                return t

        MB = R * HC * P * 4
        YB = R * TOK * 4
        r_m = region(2 * MB)
        mg = put("mg", [P, R, HC, P], F32R, r_m)
        mu = put("mu", [P, R, HC, P], F32R, r_m + MB)
        r_y = region(2 * YB)
        y0hi = put("y0hi", [P, R, TOK], F32R, r_y)
        y0lo = put("y0lo", [P, R, TOK], F32R, r_y + YB)
        md = own("md", [P, HC, D], F32R)
        r_h = region(2 * HC * HALF * 4)
        hhi = put("hhi", [P, HC, HALF], F32R, r_h)
        hlo = put("hlo", [P, HC, HALF], F32R, r_h + HC * HALF * 4)
        acc = own("acc", [P, NT, D], F32)
        r_w = region(EARLY * DC * D * 4)
        r_t = region(4 * D * 4)
        stmp = put("stmp", [P, 2, D], F32, r_t)
        htmp = put("htmp", [P, 2, D], F32, r_t + 2 * D * 4)
        r_yr = region(2 * D * 4)
        yv = put("yv", [P, 2, D], F32, r_yr)
        yT = own("yT", [P, DC, P], F32)
        su = Cursor(r_h, 2 * HC * HALF * 4)
        xp = su.put("xp", [P, NB, QW], F32)
        base = su.put("base", [P, 3, BW], F32)
        wc = su.put("wc", [P, 3, P], F32)
        cb = su.put("cb", [P, NB, CH], F32)
        diag = su.put("diag", [NB, NB, CH], F32)
        sel = su.put("sel", [NB, NT, P], F32)
        perm = su.put("perm", [P, OCT, P], BF16)
        wrep = su.put("wrep", [P, CH, KC], F32)
        prod = su.put("prod", [P, CH, KC], F32)
        w0s = su.put("w0s", [P, P], F32)
        w1s = su.put("w1s", [P, P], F32)
        cond, h1, h2 = (su.put(n, [P, NB], F32) for n in ("cond", "h1", "h2"))
        cwt, aggt = (su.put(n, [P, CH], F32) for n in ("cwt", "aggt"))
        asum = su.put("asum", [P, 3], F32)
        w2s, bkr = (su.put(n, [P, KC], F32) for n in ("w2s", "bkr"))
        tern = put("tern", [P, 3, BW], BF16, r_t)
        low = put("low", [P, BW], F32, r_t + 3 * BW * 2)
        convt = put("convt", [P, 2, R, P], F32, r_yr)
        ex = Cursor(r_m, 2 * MB)
        wring = [put(f"wring{i}", [P, DC, D], F32, r_w + i * DC * D * 4) for i in range(EARLY)]
        wring += [ex.put(f"wring{i}", [P, DC, D], F32) for i in range(EARLY, U)]
        eh = Cursor(r_h, 2 * HC * HALF * 4)
        yg = [eh.put(f"yg{i}", [P, D], F32) for i in range(U)]
        xT = [eh.put(f"xT{i}", [P, DC, P], F32) for i in range(2)]
        res = [eh.put(f"res{i}", [P, D], F32) for i in range(U)]
        fin = put("fin", [P, 2, NT, D], F32, r_y)
        cf = own("cf", [P, CF_W], F32)
        cbf = own("cbf", [P, CB_W], BF16)
        eb = own("eb", [E, D], F32)
        bd = own("bd", [P, NT, P], F32)
        gwt = own("gwt", [P, DC, E], F32)
        rec = own("rec", [P, NT, 2, 4], I32)
        rect = [own(f"rect{i}", [P, 4], I32) for i in range(U)]
        amat = own("amat", [P, NT, E], BF16)
        b01 = own("b01", [P, 2], F32)
        rows = own("rows", [1, CH + KC], F32)
        att = own("att", [NB, KC], F32)
        sm = own("sm", [NB, 4], F32)
        attx = own("attx", [P, NT, KC], F32)
        aggb = own("aggb", [P, NT], F32)
        wsc = own("wsc", [P, 3], F32)
        thr = own("thr", [P, 3], F32)
        nthr = own("nthr", [P, 3], F32)
        sud = own("sud", [P, 1], F32)
        lg = own("lg", [P, E], F32)
        mx = own("mx", [P, 8], F32)
        ix = own("ix", [P, 8], U32)
        oh = own("oh", [P, 2, E], F32)
        gap = own("gap", [P, 1], F32)
        th = own("th", [P, 1], F32)
        comb = own("comb", [P, E], F32)
        junk = own("junk", [P, E], F32)
        sidf = own("sidf", [P, 2], F32)
        sid = own("sid", [P, NT, 2], I32)
        combT = own("combT", [E, P], F32)
        cnt = own("cnt", [E, 1], F32)
        more = own("more", [E, 1], F32)
        incl = own("incl", [E, 1], F32)
        before = own("before", [E, XMAX], F32)
        lst = own("lst", [1, 2 * XMAX + 1 + XMAX], F32)
        todo = own("todo", [1, 2 * XMAX + 1], I32)

        bank = [ctx.enter_context(nc.psum_tensor(f"bank{i}", [P, 512], F32)) for i in range(8)]
        CONV = bank[0:2]
        CBB = bank[2:4]
        PG, PU = bank[2:4], bank[5:7]
        PD = (bank[4], bank[7])
        G, UU, DN = bank[0:2], bank[2:4], bank[5:7]
        BY, BT = bank[4], bank[7]
        XT, RS = bank[0:2], bank[2:4]

        def sem(name):
            return ctx.enter_context(nc.semaphore(name))

        consts_in, conds_in, base_in, rest_in = (sem(s) for s in ("consts_in", "conds_in", "base_in", "rest_in"))
        xp_in = [sem(f"xp_in{g}") for g in range(NT)]
        acc_in = sem("acc_in")
        pads_in = sem("pads_in")
        w_in = [sem(f"w_in{u}") for u in range(U)]
        dve_chain, act_chain = sem("dve_chain"), sem("act_chain")
        ctx_mm, diag_done, cb_mm, cb_done = (sem(s) for s in ("ctx_mm", "diag_done", "cb_mm", "cb_done"))
        h1_mm, h1_done, h2_mm, h2_done = (sem(s) for s in ("h1_mm", "h1_done", "h2_mm", "h2_done"))
        att_mm, att_max, att_exp, att_done = (sem(s) for s in ("att_mm", "att_max", "att_exp", "att_done"))
        attx_mm, attx_done, bd_done = (sem(s) for s in ("attx_mm", "attx_done", "bd_done"))
        asum_done, scale_mm, tern_done = (sem(s) for s in ("asum_done", "scale_mm", "tern_done"))
        pg_mm, pg_done, pu_mm, pu_done, pd_mm, pd_done = (sem(s) for s in ("pg_mm", "pg_done", "pu_mm", "pu_done", "pd_mm", "pd_done"))
        conv_mm, convt_done, y0hi_done, y0lo_done = (sem(s) for s in ("conv_mm", "convt_done", "y0hi_done", "y0lo_done"))
        g_mm, u_mm, silu_done, h_done, hhi_done, hlo_done = (sem(s) for s in ("g_mm", "u_mm", "silu_done", "h_done", "hhi_done", "hlo_done"))
        d_mm, acc_done = sem("d_mm"), sem("acc_done")
        y_mm, y_done, yt_mm, yt_done, lg_mm = (sem(s) for s in ("y_mm", "y_done", "yt_mm", "yt_done", "lg_mm"))
        y_stored = [sem(f"y_stored{i}") for i in range(2)]
        gap_done, th_done, choice_done, pos_mm, slots_done, combt_done, eb_mm, acc2_done = (
            sem(s) for s in ("gap_done", "th_done", "choice_done", "pos_mm", "slots_done", "combt_done", "eb_mm", "acc2_done"))
        recs_out = sem("recs_out")
        cnt_mm, more_done, incl_mm, before_done, list_mm, todo_done = (
            sem(s) for s in ("cnt_mm", "more_done", "incl_mm", "before_done", "list_mm", "todo_done"))
        rec_in = [sem(f"rec_in{u}") for u in range(U)]
        yg_in = [sem(f"yg_in{u}") for u in range(U)]
        res_out = [sem(f"res_out{u}") for u in range(U)]
        yg_zero, pool_steps = sem("yg_zero"), sem("pool_steps")
        xt_mm, xt_done, r_mm, res_done = (sem(s) for s in ("xt_mm", "xt_done", "r_mm", "res_done"))
        fin_in = [sem(f"fin_in{j}") for j in range(NT)]
        out_done, out_stored = sem("out_done"), sem("out_stored")

        ident = cf[:, C_ID:C_ID + P]
        iota = cf[:, C_IO:C_IO + E]
        bmask = cf[:, C_MK:C_MK + NPT]
        ones = cf[:, C_ONE:C_ONE + P]
        NCONST, NCOND, NREST = 5, 11, 5

        block = ctx.enter_context(nc.Block())

        def down_parts(g):
            return () if g < 2 else (g - 2,) if g < NT - 1 else range(NT - 3, OCT)

        @block.sync
        def _(sp):
            sp.dma_start(cond[:], a["condT"]).then_inc(conds_in, 16)
            sp.dma_start(cwt[:], a["cwT"]).then_inc(conds_in, 16)
            sp.dma_start(rows[:], a["rows"]).then_inc(conds_in, 16)
            sp.dma_start(cf[:], a["cf"]).then_inc(consts_in, 16)
            sp.dma_start(xp[:, 0:NPT], a["xp"][:, 0:NPT]).then_inc(xp_in[0], 16)
            sp.dma_start(base[:], a["base"]).then_inc(base_in, 16)
            for g in range(1, NT):
                sp.dma_start(xp[:, NPT * g:NPT * (g + 1)], a["xp"][:, NPT * g:NPT * (g + 1)]).then_inc(xp_in[g], 16)
            sp.dma_start(acc[:], a["x"].rearrange("(j p) d -> p j d", p=P)).then_inc(acc_in, 16)
            sp.dma_start(slots.rearrange("(p n) w -> p (n w)", p=P), a["pads"].to_broadcast([P, a["pads"].shape[1]])).then_inc(pads_in, 16)

            def load_w(e, u):
                sp.dma_start(wring[u][:], a["w"][bass.ds(e, 1)].rearrange("a p c d -> p (a c) d")).then_inc(w_in[u], 16)

            for u in range(EARLY):
                load_w(u, u)

            def store_y(j):
                sp.wait_ge(y_done, j + 1)
                sp.dma_start(y_tab[P * j:P * (j + 1)], yv[:, j % 2]).then_inc(y_stored[j % 2], 16)

            for j in range(TPH):
                store_y(j)
            sp.wait_ge(u_mm, 2 * HC)
            sp.wait_ge(g_mm, 2 * HC)
            for u in range(EARLY, U):
                load_w(u, u)
            for j in range(TPH, NT):
                store_y(j)

            def load_rec(chunk, e, u):
                sp.dma_start(rect[u][:], slots_v[bass.ds(chunk, 1), :, bass.ds(e, 1), :].rearrange("c p e w -> (c p) (e w)")).then_inc(rec_in[u], 16)

            sp.wait_ge(recs_out, 2 * NT * 16)
            for u in range(U):
                load_rec(0, u, u)
            with sp.Fori(1, G0) as g:
                for u in range(U):
                    sp.wait_ge(r_mm, g * U + (u - U + 1))
                    load_w(g * U + u, u)
                    sp.wait_ge(res_out[u], g * 16)
                    load_rec(0, g * U + u, u)
            sp.wait_ge(todo_done, 1)
            bodies = sp.value_load(todo[0:1, 2 * XMAX:2 * XMAX + 1], min_val=0, max_val=XMAX // XU)
            with sp.If(bodies > 0):
                with sp.Fori(0, bodies) as g:
                    for u in range(XU):
                        e = sp.value_load(todo[0:1, bass.ds(g * XU + u, 1)], min_val=0, max_val=E - 1)
                        c = sp.value_load(todo[0:1, bass.ds(g * XU + (u + XMAX), 1)], min_val=0, max_val=CHUNKS)
                        sp.wait_ge(r_mm, g * XU + (E + u - XU + 1))
                        load_w(e, u)
                        sp.wait_ge(res_out[u], g * 16 + G0 * 16)
                        load_rec(c, e, u)
            for u in range(U):
                sp.wait_ge(res_out[u], bodies * 16 + G0 * 16 if u < XU else G0 * 16)
                if u < XU:
                    sp.nop()
            for j in range(NT):
                for k in range(2):
                    sp.dma_start(fin[:, k, j], picked[(k * NT + j) * P:(k * NT + j + 1) * P]).then_inc(fin_in[j], 16)
            for j in range(NT):
                sp.wait_ge(out_done, j + 1)
                sp.dma_start(a["out"][P * j:P * (j + 1)], acc[:, j]).then_inc(out_stored, 16)
            sp.wait_ge(out_stored, NT * 16)

        @block.gpsimd
        def _(pool):
            for g in range(NT):
                pool.wait_ge(y0hi_done, g + 1)
                nc.gpsimd.tensor_tensor(y0lo[:, :, P * g:P * (g + 1)], convt[:, g % 2], y0hi[:, :, P * g:P * (g + 1)].bitcast(F32), ALU.subtract).then_inc(y0lo_done, 1)
            pool.wait_ge(pads_in, 16)
            pool.wait_ge(rest_in, NREST * 16)
            for j in range(NT):
                pool.wait_ge(slots_done, j + 1)
                for k in range(2):
                    pool.indirect_dma_start(out=slots, out_offset=bass.IndirectOffsetOnAxis(ap=sid[:, j, k:k + 1], axis=0),
                                            in_=rec[:, j, k], in_offset=None).then_inc(recs_out, 16)
            pool.wait_ge(d_mm, NT)
            for u in range(U):
                nc.gpsimd.memset(yg[u][:], 0.0).then_inc(yg_zero, 1)
            pool.wait_ge(yg_zero, U)
            for i in range(2):
                pool.wait_ge(y_stored[i], NT // 2 * 16)

            last_token, last_row = pool.to_reg(TOK - 1), pool.to_reg(2 * TOK - 1)

            def gather(g, u, used=None):
                pool.wait_ge(rec_in[u], (g + 1) * 16)
                if used is not None:
                    pool.wait_ge(xt_mm, used)
                pool.sem_inc(pool_steps, 1)
                pool.indirect_dma_start(out=yg[u][:], out_offset=None, in_=y_tab,
                                        in_offset=bass.IndirectOffsetOnAxis(ap=rect[u][:, 0:1].bitcast(U32), axis=0),
                                        bounds_check=last_token, oob_is_err=False).then_inc(yg_in[u], 16)

            def scatter(i, u):
                pool.wait_ge(res_done, i + 1)
                pool.sem_inc(pool_steps, 1)
                pool.indirect_dma_start(out=picked, out_offset=bass.IndirectOffsetOnAxis(ap=rect[u][:, 1:2].bitcast(U32), axis=0),
                                        in_=res[u][:], in_offset=None,
                                        bounds_check=last_row, oob_is_err=False).then_inc(res_out[u], 16)

            for u in range(U):
                gather(0, u)
                if u >= LAG:
                    scatter(u - LAG, u - LAG)
            with pool.Fori(1, G0) as g:
                for u in range(U):
                    gather(g, u, g * U + (u - U + 1))
                    scatter(g * U + (u - LAG), (u - LAG) % U)
            for t in range(E - LAG, E):
                scatter(t, t % U)
            pool.wait_ge(todo_done, 1)
            bodies = pool.value_load(todo[0:1, 2 * XMAX:2 * XMAX + 1], min_val=0, max_val=XMAX // XU)
            with pool.If(bodies > 0):
                with pool.Fori(0, bodies) as g:
                    for u in range(XU):
                        gather(g + G0, u, g * XU + (E + u - XU + 1))
                    for u in range(XU):
                        scatter(g * XU + (E + u), u)

        @block.scalar
        def _(act):
            chain = [0]

            def link(ins):
                chain[0] += 1
                ins.then_inc(act_chain, 1)
                act.wait_ge(act_chain, chain[0])

            for t, k in ((b01, "b01"), (w0s, "w0"), (w1s, "w1"), (w2s, "w2"), (sel, "sel"), (wrep, "wrep"), (bkr, "bkr"), (gwt, "gwT")):
                act.dma_start(t[:], a[k]).then_inc(conds_in, 16)
            for t, k in ((perm, "perm"), (cbf, "cb")):
                act.dma_start(t[:], a[k].bitcast(BF16)).then_inc(consts_in, 16)
            for t, k in ((wc, "wc"), (eb, "eb")):
                act.dma_start(t[:], a[k]).then_inc(consts_in, 16)
            act.dma_start(rec[:], a["rec"]).then_inc(rest_in, 16 * NREST)
            for hm, bcol, h, hd in ((h1_mm, 0, h1, h1_done), (h2_mm, 1, h2, h2_done)):
                act.wait_ge(hm, 1)
                nc.scalar.activation(h[:], BY[:, NB * bcol:NB * (bcol + 1)], ACT.Gelu, bias=b01[:, bcol:bcol + 1]).then_inc(hd, 1)
                if bcol == 0:
                    act.wait_ge(base_in, 16)
                    for m in range(3):
                        if m:
                            act.wait_ge(asum_done, m)
                        nc.scalar.activation(low[:], base[:, m], ACT.Abs, accum_out=asum[:, m:m + 1]).then_inc(asum_done, 1)
                    act.wait_ge(cb_mm, 1)
                    for h_ in range(2):
                        nc.scalar.activation(cb[:].rearrange("p n c -> p (n c)")[:, 512 * h_:512 * (h_ + 1)], CBB[h_][:], ACT.Copy).then_inc(cb_done, 1)

            act.wait_ge(att_max, 1)
            nc.scalar.activation(att[:], BY[0:NB, 64:64 + KC], ACT.Exp, bias=sm[:, 1:2], accum_out=sm[:, 2:3]).then_inc(att_exp, 1)

            def conv_hi(g):
                act.wait_ge(convt_done, g + 1)
                nc.scalar.activation(y0hi[:, :, P * g:P * (g + 1)], convt[:, g % 2], ACT.Copy).then_inc(y0hi_done, 1)

            def gate_table(k):
                act.wait_ge(pg_mm, k + 1)
                for h_ in range(2):
                    v = nc.scalar.activation(mg[:, 2 * h_:2 * h_ + 2, :, OB * k:OB * (k + 1)],
                                             PG[h_][:, 0:BW // 2].rearrange("p (r c o) -> p r c o", r=2, o=OB), ACT.Copy)
                v.then_inc(pg_done, 1)

            def down_table(k):
                act.wait_ge(pd_mm, k + 1)
                for h_, (c0, c1) in enumerate(((0, 6), (6, HC))):
                    v = nc.scalar.activation(md[:, c0:c1, OUT8 * k:OUT8 * (k + 1)],
                                             PD[h_][:, 0:(c1 - c0) * OUT8].rearrange("p (c o) -> p c o", o=OUT8), ACT.Copy)
                v.then_inc(pd_done, 1)

            for g in range(NT):
                conv_hi(g)
                gate_table(g)
                for k in down_parts(g):
                    down_table(k)
                if g == 1:
                    act.wait_ge(attx_mm, 1)
                    nc.scalar.activation(attx[:].rearrange("p g k -> p (g k)"), BT[:, 64:64 + NT * KC], ACT.Copy).then_inc(attx_done, 1)

            def silu(n):
                act.wait_ge(g_mm, n + 1)
                if n >= 2:
                    act.wait_ge(h_done, n - 1)
                nc.scalar.activation(stmp[:, n % 2], G[n % 2][:], ACT.Silu, scale=wsc[:, 0:1]).then_inc(silu_done, 1)

            def hid_hi(n):
                act.wait_ge(h_done, n + 1)
                nc.scalar.activation(hhi[:, n % HC], htmp[:, n % 2], ACT.Copy).then_inc(hhi_done, 1)

            def y_evac(j):
                act.wait_ge(y_mm, j + 1)
                if j == 0:
                    act.wait_ge(y0lo_done, NT)
                if j >= 2:
                    act.wait_ge(y_stored[j % 2], j // 2 * 16)
                    act.wait_ge(yt_mm, j - 1)
                nc.scalar.activation(yv[:, j % 2], BY[:], ACT.Identity, bias=aggb[:, j:j + 1]).then_inc(y_done, 1)

            def yt_evac(j):
                act.wait_ge(yt_mm, j + 1)
                if j >= 1:
                    act.wait_ge(lg_mm, j)
                nc.scalar.activation(yT[:].rearrange("p c t -> p (c t)"), BT[:], ACT.Copy).then_inc(yt_done, 1)

            def weight_tanh(j):
                act.wait_ge(gap_done, j + 1)
                nc.scalar.activation(th[:], gap[:], ACT.Tanh, scale=0.5).then_inc(th_done, 1)

            act.wait_ge(tern_done, 3)
            for half in range(2):
                for c in range(HC):
                    n = half * HC + c
                    silu(n)
                    if c >= 1:
                        hid_hi(n - 1)
                    if half == 1:
                        j = TPH - 1
                        if c == 0:
                            y_evac(j)
                        if c == 1:
                            yt_evac(j)
                        if c == 3:
                            weight_tanh(j)
                hid_hi(half * HC + HC - 1)
                for t in range(1, TPH + half):
                    j = half * TPH + t - 1
                    y_evac(j)
                    yt_evac(j)
                    weight_tanh(j)

            def evac(i, g, u, first=False):
                act.wait_ge(rec_in[u], (g + 1) * 16)
                act.wait_ge(r_mm, i + 1)
                if not first:
                    act.wait_ge(res_out[u], g * 16)
                nc.scalar.activation(res[u][:], RS[u % 2][:], ACT.Copy, scale=rect[u][:, 2:3].bitcast(F32)).then_inc(res_done, 1)

            for u in range(U):
                evac(u, 0, u, True)
            with act.Fori(1, G0) as g:
                for u in range(U):
                    evac(g * U + u, g, u)
            act.wait_ge(todo_done, 1)
            bodies = act.value_load(todo[0:1, 2 * XMAX:2 * XMAX + 1], min_val=0, max_val=XMAX // XU)
            with act.If(bodies > 0):
                with act.Fori(0, bodies) as g:
                    for u in range(XU):
                        evac(g * XU + (E + u), g + G0, u)

        @block.vector
        def _(dve):
            chain = [0]

            def link(ins):
                chain[0] += 1
                ins.then_inc(dve_chain, 1)
                dve.wait_ge(dve_chain, chain[0])

            dve.wait_ge(consts_in, NCONST * 16)
            dve.wait_ge(ctx_mm, 1)
            nc.vector.tensor_tensor(diag[:], BT[0:NB, 0:CH].unsqueeze(1).to_broadcast([NB, NB, CH]),
                                    ident[0:NB, 0:NB].unsqueeze(2).to_broadcast([NB, NB, CH]), ALU.mult).then_inc(diag_done, 1)
            dve.wait_ge(scale_mm, 1)
            nc.vector.tensor_scalar(wsc[:], BT[:, 32:35], 1.0 / (OCT * HID8 * IN8), None, ALU.mult).then_inc(dve_chain, 1)
            chain[0] += 1
            dve.wait_ge(dve_chain, chain[0])
            nc.vector.tensor_scalar(thr[:], wsc[:], 0.5, None, ALU.mult).then_inc(dve_chain, 1)
            nc.vector.tensor_scalar(nthr[:], wsc[:], -0.5, None, ALU.mult).then_inc(dve_chain, 1)
            nc.vector.tensor_tensor(sud[:], wsc[:, 1:2], wsc[:, 2:3], ALU.mult).then_inc(dve_chain, 1)
            chain[0] += 3
            dve.wait_ge(dve_chain, chain[0])

            def quantize(m):
                link(nc.vector.tensor_scalar(low[:], base[:, m], nthr[:, m:m + 1], None, ALU.is_lt))
                nc.vector.scalar_tensor_tensor(tern[:, m], base[:, m], thr[:, m:m + 1], low[:], ALU.is_gt, ALU.subtract).then_inc(tern_done, 1)
                dve.wait_ge(tern_done, m + 1)

            def conv_evac(g):
                dve.wait_ge(conv_mm, g + 1)
                if g == 0:
                    dve.wait_ge(cb_done, 2)
                if g >= 2:
                    dve.wait_ge(y0hi_done, g - 1)
                    dve.wait_ge(y0lo_done, g - 1)
                nc.vector.tensor_tensor(convt[:, g % 2].rearrange("p r (n c) -> p r n c", c=CH),
                                        CONV[g % 2][:].rearrange("p (n r c) -> p r n c", n=NPT, c=CH),
                                        cb[:, NPT * g:NPT * (g + 1)].unsqueeze(1).to_broadcast([P, R, NPT, CH]), ALU.add).then_inc(convt_done, 1)

            def up_table(k):
                dve.wait_ge(pu_mm, k + 1)
                for h_ in range(2):
                    v = nc.vector.tensor_copy(mu[:, 2 * h_:2 * h_ + 2, :, OB * k:OB * (k + 1)],
                                              PU[h_][:, 0:BW // 2].rearrange("p (r c o) -> p r c o", r=2, o=OB))
                v.then_inc(pu_done, 1)

            quantize(0)
            quantize(1)
            for g in range(NT):
                conv_evac(g)
                up_table(g)
                if g == 0:
                    quantize(2)
                    dve.wait_ge(att_mm, 1)
                    link(nc.vector.reduce_max(sm[:, 0:1], BY[0:NB, 64:64 + KC], axis=AX.X))
                    nc.vector.tensor_scalar(sm[:, 1:2], sm[:, 0:1], -1.0, None, ALU.mult).then_inc(att_max, 1)
                    dve.wait_ge(att_exp, 1)
                    link(nc.vector.reciprocal(sm[:, 3:4], sm[:, 2:3]))
                    nc.vector.tensor_scalar(att[:], att[:], sm[:, 3:4], None, ALU.mult).then_inc(att_done, 1)
                if g == 1:
                    dve.wait_ge(attx_done, 1)
                    link(nc.vector.tensor_tensor(prod[:, 0:NT, :], attx[:], bkr[:].unsqueeze(1).to_broadcast([P, NT, KC]), ALU.mult))
                    link(nc.vector.tensor_reduce(aggb[:], prod[:, 0:NT, :], AX.X, ALU.add))
                if g >= 1:
                    for t in ((g - 1, NT - 1) if g == NT - 1 else (g - 1,)):
                        link(nc.vector.tensor_tensor(prod[:], wrep[:], attx[:, t].unsqueeze(1).to_broadcast([P, CH, KC]), ALU.mult))
                        link(nc.vector.tensor_reduce(aggt[:], prod[:], AX.X, ALU.add))
                        link(nc.vector.tensor_tensor(bd[:, t].rearrange("p (b o) -> p b o", b=NPT),
                                                     aggt[:].unsqueeze(1).to_broadcast([P, NPT, CH]),
                                                     bmask.unsqueeze(2).to_broadcast([P, NPT, CH]), ALU.mult))

            def hidden(n):
                dve.wait_ge(silu_done, n + 1)
                dve.wait_ge(u_mm, n + 1)
                if n >= 2:
                    dve.wait_ge(hhi_done, n - 1)
                    dve.wait_ge(hlo_done, n - 1)
                nc.vector.tensor_tensor(htmp[:, n % 2], UU[n % 2][:], stmp[:, n % 2], ALU.mult).then_inc(h_done, 1)

            def hid_lo(n):
                dve.wait_ge(hhi_done, n + 1)
                nc.vector.tensor_tensor(hlo[:, n % HC], htmp[:, n % 2], hhi[:, n % HC].bitcast(F32), ALU.subtract).then_inc(hlo_done, 1)

            def acc_evac(j):
                if j == 0:
                    dve.wait_ge(acc_in, 16)
                dve.wait_ge(d_mm, j + 1)
                nc.vector.scalar_tensor_tensor(acc[:, j], DN[j % 2][:], sud[:, 0:1], acc[:, j], ALU.mult, ALU.add).then_inc(acc_done, 1)

            def choose(j):
                dve.wait_ge(lg_mm, j + 1)
                link(nc.vector.max(mx[:], BY[:, 0:E]))
                nc.vector.tensor_tensor(gap[:], mx[:, 0:1], mx[:, 1:2], ALU.subtract).then_inc(gap_done, 1)
                link(nc.vector.max_index(ix[:], mx[:], BY[:, 0:E]))
                for k in range(2):
                    link(nc.vector.tensor_scalar(oh[:, k], iota, ix[:, k:k + 1], None, ALU.is_equal))
                link(nc.vector.tensor_tensor(amat[:, j], oh[:, 0], oh[:, 1], ALU.add))

            def weigh(j):
                dve.wait_ge(th_done, j + 1)
                for k, s in ((0, 0.5), (1, -0.5)):
                    link(nc.vector.tensor_scalar(rec[:, j, k, 2:3].bitcast(F32), th[:], s, 0.5, ALU.mult, ALU.add))
                link(nc.vector.tensor_scalar(comb[:], oh[:, 0], rec[:, j, 0, 2:3].bitcast(F32), None, ALU.mult))
                nc.vector.scalar_tensor_tensor(comb[:], oh[:, 1], rec[:, j, 1, 2:3].bitcast(F32), comb[:], ALU.mult, ALU.add).then_inc(choice_done, 1)

            def place(j):
                dve.wait_ge(pos_mm, j + 1)
                nc.vector.tensor_copy(combT[:], BY[0:E, 64:64 + P]).then_inc(combt_done, 1)
                link(nc.vector.scalar_tensor_tensor(lg[:], BY[:, E:2 * E], float(E), iota, ALU.mult, ALU.add))
                for k in range(2):
                    link(nc.vector.scalar_tensor_tensor(junk[:], iota, ix[:, k:k + 1], lg[:], ALU.is_equal, ALU.mult, accum_out=sidf[:, k:k + 1]))
                nc.vector.tensor_copy(sid[:, j], sidf[:]).then_inc(slots_done, 1)
                dve.wait_ge(slots_done, j + 1)

            def add_bias(j):
                dve.wait_ge(eb_mm, j + 1)
                nc.vector.tensor_tensor(acc[:, j], acc[:, j], BT[:], ALU.add).then_inc(acc2_done, 1)

            dve.wait_ge(rest_in, NREST * 16)
            for half in range(2):
                for c in range(HC):
                    n = half * HC + c
                    hidden(n)
                    if c >= 1:
                        hid_lo(n - 1)
                    if half == 1:
                        j = TPH - 1
                        if c == 2:
                            choose(j)
                        if c == 3:
                            weigh(j)
                        if c == 4:
                            place(j)
                        if c == 5:
                            add_bias(j)
                hid_lo(half * HC + HC - 1)
                acc_evac(half * TPH)
                for t in range(1, TPH + half):
                    j = half * TPH + t - 1
                    choose(j)
                    weigh(j)
                    place(j)
                    add_bias(j)
                    if t < TPH:
                        acc_evac(j + 1)

            def xt_evac(i, u, first=False):
                dve.wait_ge(xt_mm, i + 1)
                if not first:
                    dve.wait_ge(r_mm, i - 1)
                nc.vector.tensor_copy(xT[u % 2][:].rearrange("p c t -> p (c t)"), XT[u % 2][:]).then_inc(xt_done, 1)

            xt_evac(0, 0, True)
            xt_evac(1, 1, True)
            dve.wait_ge(cnt_mm, 1)
            link(nc.vector.tensor_copy(cnt[:], BY[0:E, 0:1]))
            nc.vector.tensor_scalar(junk[0:E, 0:8], cf[0:E, C_THR:C_THR + 8], cnt[:, 0:1], 0.0, ALU.is_lt, ALU.add, accum_out=more[:]).then_inc(more_done, 1)
            dve.wait_ge(incl_mm, 1)
            link(nc.vector.tensor_copy(incl[:], BY[0:E, 0:1]))
            nc.vector.tensor_scalar(before[:], iota[0:E, 0:XMAX], incl[:, 0:1], None, ALU.is_ge).then_inc(before_done, 1)
            dve.wait_ge(list_mm, 1)
            ends = lst[:, 2 * XMAX + 1:]
            link(nc.vector.tensor_copy(lst[:, 0:2 * XMAX + 1], BY[0:1, 0:2 * XMAX + 1]))
            link(nc.vector.tensor_scalar(ends, lst[:, 0:XMAX], float(E), None, ALU.is_ge))
            link(nc.vector.tensor_tensor(lst[:, 0:XMAX], lst[:, 0:XMAX], ends, ALU.subtract))
            link(nc.vector.scalar_tensor_tensor(lst[:, XMAX:2 * XMAX], iota[0:1, 0:XMAX], 1.0, lst[:, XMAX:2 * XMAX], ALU.add, ALU.subtract))
            link(nc.vector.scalar_tensor_tensor(junk[0:1, 0:XMAX], ends, float(CHUNKS), lst[:, XMAX:2 * XMAX], ALU.mult, ALU.max))
            link(nc.vector.tensor_copy(lst[:, XMAX:2 * XMAX], junk[0:1, 0:XMAX]))
            link(nc.vector.tensor_scalar(junk[0:1, 0:XMAX // XU], cf[0:1, C_IO:C_IO + XMAX:XU], lst[:, 2 * XMAX:2 * XMAX + 1], 0.0, ALU.is_lt, ALU.add,
                                         accum_out=lg[0:1, 0:1]))
            nc.vector.tensor_copy(todo[:, 2 * XMAX:2 * XMAX + 1], lg[0:1, 0:1]).then_inc(dve_chain, 1)
            chain[0] += 1
            link(nc.vector.tensor_copy(todo[:, 0:2 * XMAX], lst[:, 0:2 * XMAX]))
            nc.vector.engine_nop().then_inc(todo_done, 1)
            for u in range(2, U):
                xt_evac(u, u)

            with dve.Fori(1, G0) as g:
                for u in range(U):
                    xt_evac(g * U + u, u)
            bodies = dve.value_load(todo[0:1, 2 * XMAX:2 * XMAX + 1], min_val=0, max_val=XMAX // XU)
            with dve.If(bodies > 0):
                with dve.Fori(0, bodies) as g:
                    for u in range(XU):
                        xt_evac(g * XU + (E + u), u)
            for j in range(NT):
                dve.wait_ge(fin_in[j], 32)
                link(nc.vector.tensor_tensor(acc[:, j], acc[:, j], fin[:, 0, j], ALU.add))
                nc.vector.tensor_tensor(acc[:, j], acc[:, j], fin[:, 1, j], ALU.add).then_inc(out_done, 1)

        @block.tensor
        def _(pe):
            mm = nc.tensor.matmul

            pe.wait_ge(conds_in, NCOND * 16)
            pe.wait_ge(consts_in, NCONST * 16)
            mm(BT[0:NB, 0:CH], cond[:], cwt[:], start=True, stop=False)
            mm(BT[0:NB, 0:CH], ones[0:1, 0:NB], rows[:, 0:CH], start=False, stop=True).then_inc(ctx_mm, 1)
            mm(BY[:, 0:NB], w0s[:], cond[:], start=True, stop=True).then_inc(h1_mm, 1)
            pe.wait_ge(diag_done, 1)
            for h_ in range(2):
                v = mm(CBB[h_][:], ones[0:NB, :], diag[:].rearrange("b n c -> b (n c)")[:, 512 * h_:512 * (h_ + 1)], start=True, stop=True)
            v.then_inc(cb_mm, 1)

            def conv(g):
                pe.wait_ge(xp_in[g], 16)
                if g >= 2:
                    pe.wait_ge(convt_done, g - 1)
                for b in range(NPT):
                    for s in range(3):
                        v = mm(CONV[g % 2][:, P * b:P * (b + 1)], xp[:, NPT * g + b, s:s + P], wc[:, s], start=(s == 0), stop=(s == 2))
                v.then_inc(conv_mm, 1)

            def table(k, m, banks, made, used):
                if k >= 1:
                    pe.wait_ge(used, k)
                cut = BW // 2 if m < 2 else 6 * OUT8
                for h_, (c0, c1) in enumerate(((0, cut), (cut, BW))):
                    v = mm(banks[h_][:, 0:c1 - c0], perm[:, k], tern[:, m, c0:c1], start=True, stop=True)
                v.then_inc(made, 1)

            pe.wait_ge(asum_done, 3)
            mm(BT[:, 32:35], ones, asum[:], start=True, stop=True).then_inc(scale_mm, 1)
            pe.wait_ge(h1_done, 1)
            mm(BY[:, NB:2 * NB], w1s[:], h1[:], start=True, stop=True).then_inc(h2_mm, 1)
            conv(0)
            pe.wait_ge(h2_done, 1)
            mm(BY[0:NB, 64:64 + KC], h2[:], w2s[:], start=True, stop=False)
            mm(BY[0:NB, 64:64 + KC], ones[0:1, 0:NB], rows[:, CH:CH + KC], start=False, stop=True).then_inc(att_mm, 1)
            pe.wait_ge(cb_done, 2)
            for g in range(NT):
                if g >= 1:
                    conv(g)
                if g == 0:
                    pe.wait_ge(tern_done, 2)
                table(g, 0, PG, pg_mm, pg_done)
                table(g, 1, PU, pu_mm, pu_done)
                if g == 1:
                    pe.wait_ge(att_done, 1)
                    for t in range(NT):
                        v = mm(BT[:, 64 + KC * t:64 + KC * (t + 1)], sel[:, t], att[:], start=True, stop=True)
                    v.then_inc(attx_mm, 1)
                if g == 2:
                    pe.wait_ge(attx_done, 1)
                    pe.wait_ge(tern_done, 3)
                for k in down_parts(g):
                    table(k, 2, PD, pd_mm, pd_done)
            pe.wait_ge(pg_done, OCT)
            pe.wait_ge(pu_done, OCT)

            def hidden(n, half):
                c = n % HC
                if n % HC == 0:
                    pe.wait_ge(y0hi_done, (half + 1) * TPH)
                    pe.wait_ge(y0lo_done, (half + 1) * TPH)
                for banks, tab, used, made in ((G, mg, silu_done, g_mm), (UU, mu, h_done, u_mm)):
                    if n >= 2:
                        pe.wait_ge(used, n - 1)
                    for r in range(R):
                        for part, y in enumerate((y0hi, y0lo)):
                            v = mm(banks[n % 2][:], tab[:, r, c], y[:, r, HALF * half:HALF * (half + 1)],
                                   start=(r == 0 and part == 0), stop=(r == R - 1 and part == 1))
                    v.then_inc(made, 1)

            def layer2_y(j):
                pe.wait_ge(acc_done, j + 1)
                if j >= 1:
                    pe.wait_ge(slots_done, j)
                mm(BY[:], bd[:, j], acc[:, j], start=True, stop=True).then_inc(y_mm, 1)

            def layer2_yt(j):
                pe.wait_ge(y_done, j + 1)
                if j >= 1:
                    pe.wait_ge(acc2_done, j)
                for c in range(DC):
                    v = nc.tensor.transpose(BT[:, P * c:P * (c + 1)], yv[:, j % 2, P * c:P * (c + 1)], ident)
                v.then_inc(yt_mm, 1)

            def layer2_logits(j):
                pe.wait_ge(yt_done, j + 1)
                for c in range(DC):
                    v = mm(BY[:, 0:E], yT[:, c], gwt[:, c], start=(c == 0), stop=(c == DC - 1))
                v.then_inc(lg_mm, 1)

            def layer2_positions(j):
                pe.wait_ge(choice_done, j + 1)
                for t in range(j):
                    mm(BY[:, E:2 * E], cbf[:, B_ONE:B_ONE + P], amat[:, t], start=(t == 0), stop=False)
                mm(BY[:, E:2 * E], cbf[:, B_UP:B_UP + P], amat[:, j], start=(j == 0), stop=True)
                nc.tensor.transpose(BY[0:E, 64:64 + P], comb[:], ident).then_inc(pos_mm, 1)

            def layer2_bias(j):
                pe.wait_ge(combt_done, j + 1)
                mm(BT[:], combT[:], eb[:], start=True, stop=True).then_inc(eb_mm, 1)

            layer2 = (layer2_y, layer2_yt, layer2_logits, layer2_positions, layer2_bias)

            def down(j, steps):
                half, t = divmod(j, TPH)
                if j >= 2:
                    pe.wait_ge(acc_done, j - 1)
                for c in range(HC):
                    if t == 0:
                        pe.wait_ge(hhi_done, half * HC + c + 1)
                        pe.wait_ge(hlo_done, half * HC + c + 1)
                    for part, h in enumerate((hhi, hlo)):
                        v = mm(DN[j % 2][:], h[:, c, P * t:P * (t + 1)], md[:, c], start=(c == 0 and part == 0), stop=(c == HC - 1 and part == 1))
                    if steps and c % 2 == 1:
                        layer2[c // 2](j - 1)
                v.then_inc(d_mm, 1)

            for half in range(2):
                for c in range(HC):
                    hidden(half * HC + c, half)
                    if half == 1 and c < len(layer2):
                        layer2[c](TPH - 1)
                pe.wait_ge(pd_done, OCT)
                for t in range(TPH):
                    down(half * TPH + t, t >= 1)
            for step in layer2:
                step(NT - 1)

            def transposes(g, u, i, first=False):
                pe.wait_ge(yg_in[u], (g + 1) * 16)
                if not first:
                    pe.wait_ge(xt_done, i - 1)
                for c in range(DC):
                    v = nc.tensor.transpose(XT[u % 2][:, P * c:P * (c + 1)], yg[u][:, P * c:P * (c + 1)], ident)
                v.then_inc(xt_mm, 1)

            def product(g, u, i, first=False):
                pe.wait_ge(xt_done, i + 1)
                pe.wait_ge(w_in[u], (g + 1) * 16)
                if not first:
                    pe.wait_ge(res_done, i - 1)
                for c in range(DC):
                    v = mm(RS[u % 2][:], xT[u % 2][:, c], wring[u][:, c], start=(c == 0), stop=(c == DC - 1))
                v.then_inc(r_mm, 1)

            transposes(0, 0, 0, True)
            for j in range(NT):
                v = mm(BY[0:E, 0:1], amat[:, j], cbf[:, B_ONE:B_ONE + 1], start=(j == 0), stop=(j == NT - 1))
            v.then_inc(cnt_mm, 1)
            transposes(0, 1, 1, True)
            product(0, 0, 0, True)
            pe.wait_ge(more_done, 1)
            mm(BY[0:E, 0:1], cf[0:E, C_TRI:C_TRI + E], more[:], start=True, stop=True).then_inc(incl_mm, 1)
            pe.wait_ge(before_done, 1)
            mm(BY[0:1, 0:XMAX], ones[0:E, 0:1], before[:], start=True, stop=True)
            mm(BY[0:1, XMAX:2 * XMAX], more[:], before[:], start=True, stop=True)
            mm(BY[0:1, 2 * XMAX:2 * XMAX + 1], more[:], ones[0:E, 0:1], start=True, stop=True).then_inc(list_mm, 1)
            for u in range(2, U):
                transposes(0, u, u)
                product(0, u - 1, u - 1, u - 1 < 2)

            with pe.Fori(1, G0) as g:
                for u in range(U):
                    transposes(g, u, g * U + u)
                    if u == 0:
                        product(g - 1, U - 1, g * U - 1)
                    else:
                        product(g, u - 1, g * U + (u - 1))
            product(G0 - 1, U - 1, E - 1)
            pe.wait_ge(todo_done, 1)
            bodies = pe.value_load(todo[0:1, 2 * XMAX:2 * XMAX + 1], min_val=0, max_val=XMAX // XU)
            with pe.If(bodies > 0):
                with pe.Fori(0, bodies) as g:
                    for u in range(XU):
                        transposes(g + G0, u, g * XU + (E + u))
                    for u in range(XU):
                        product(g + G0, u, g * XU + (E + u))


def layouts(i):
    import numpy as np

    f = np.float32
    x = i["x"]
    out = {}
    xp = np.zeros((R, CH, NB, QW), f)
    xp[:, :, :, 1:1 + P] = x.reshape(NB, CH, P, R).transpose(3, 1, 0, 2)
    out["xp"] = xp.reshape(P, NB, QW)
    out["x"] = x.reshape(TOK, D)
    cw = i["L0_cond_weight"]
    per = CH // 4
    wc = np.zeros((R, CH, 3, R, CH), f)
    for s in range(R):
        for d in range(3):
            for r in range(R):
                tap = 4 * (d - 1) + s - r + 4
                if 0 <= tap < TAPS:
                    for co in range(CH):
                        g0 = co // per * per
                        wc[s, g0:g0 + per, d, r, co] = cw[co, :, tap]
    out["wc"] = wc.reshape(P, 3, P)

    def hidden_pad(w, axis):
        shape = list(w.shape)
        shape[axis] = HC * OB
        p = np.zeros(shape, f)
        p[tuple(slice(0, n) for n in w.shape)] = w
        return p

    base = np.zeros((P, 3, BW), f)
    for m, k in enumerate(("L0_ffn_w_gate", "L0_ffn_w_up")):
        w = hidden_pad(i[k], 1).reshape(OCT, HC * OB, OB, R)
        base[:, m] = w.transpose(0, 2, 3, 1).reshape(P, BW)
    w = hidden_pad(i["L0_ffn_w_down"], 2).reshape(OCT, OUT8, HC, OB)
    base[:, 2] = w.transpose(0, 3, 2, 1).reshape(P, BW)
    out["base"] = base
    out["condT"] = i["cond_128"].T
    out["cwT"] = i["L0_cond_c_weight"].T
    out["rows"] = np.concatenate([i["fside_S_0"], i["L1_cond_b2"]])[None]
    out["b01"] = np.stack([i["L1_cond_b0"], i["L1_cond_b1"]], 1)
    out["w0"], out["w1"], out["w2"] = i["L1_cond_W0"], i["L1_cond_W1"], i["L1_cond_W2"]
    out["wrep"] = np.tile(i["L1_cond_weight"][..., 0].transpose(2, 1, 0), (NPT, 1, 1))
    out["bkr"] = np.tile(i["L1_cond_bias_k"].T, (NPT, 1))
    out["gwT"] = i["L1_ffn_gate_w"].T.reshape(DC, P, E).transpose(1, 0, 2)
    out["w"] = i["L1_ffn_expert_w"].reshape(E, D, DC, P).transpose(0, 3, 2, 1)
    out["eb"] = i["L1_ffn_expert_b"]

    def bf16_bits(v):
        return (np.ascontiguousarray(v).view(np.uint32) >> 16).astype(np.uint16)

    sel = np.zeros((NB, NT, P), f)
    for b in range(NB):
        sel[b, b // NPT, b % NPT * CH:(b % NPT + 1) * CH] = 1
    out["sel"] = sel
    S = np.zeros((OCT, OCT, OCT), f)
    S[0, 0, 0] = 1
    for n in range(1, OCT):
        S[0, n, n] = S[n, 0, n] = 1
        S[n, n, 0] = -1
    for t in ((1, 2, 3), (1, 4, 5), (1, 7, 6), (2, 4, 6), (2, 5, 7), (3, 4, 7), (3, 6, 5)):
        for v in range(3):
            p_, q_, r_ = t[v], t[(v + 1) % 3], t[(v + 2) % 3]
            S[p_, q_, r_], S[q_, p_, r_] = 1, -1
    perm = np.zeros((OCT, OB, OCT, OCT, OB), f)
    for j in range(OCT):
        for n in range(OCT):
            for k in range(OCT):
                for d in range(OB):
                    perm[j, d, k, n, d] = S[j, n, k]
    out["perm"] = bf16_bits(perm.reshape(P, OCT, P))
    cf = np.zeros((P, CF_W), f)
    cf[:, C_ID:C_ID + P] = np.eye(P)
    cf[:, C_IO:C_IO + E] = np.arange(E)
    cf[:, C_MK:C_MK + NPT] = np.arange(P)[:, None] // CH == np.arange(NPT)
    cf[0:E, C_TRI:C_TRI + E] = np.triu(np.ones((E, E)))
    cf[:, C_THR:C_THR + 8] = np.append(np.arange(1, CHUNKS) * P, 2 * TOK)
    cf[:, C_ONE:C_ONE + P] = 1
    out["cf"] = cf
    cb = np.ones((P, CB_W), f)
    cb[:, B_UP:B_UP + P] = np.triu(np.ones((P, P)), 1)
    out["cb"] = bf16_bits(cb)
    rec = np.zeros((P, NT, 2, 4), np.int32)
    tok = np.arange(TOK).reshape(NT, P).T
    rec[:, :, :, 0] = tok[:, :, None]
    rec[:, :, :, 1] = tok[:, :, None] + np.array([0, TOK])
    out["rec"] = rec
    pads = np.zeros(((CHUNKS + 1) * E, 4), np.int32)
    pads[:, 0:2] = PADROW
    out["pads"] = pads.reshape(1, -1)
    return {k: np.ascontiguousarray(v) for k, v in out.items()}


def kernel(**inputs):
    import numpy as np
    import concourse.bacc as bacc
    from concourse.bass_utils import run_bass_kernel_spmd

    arrays = layouts({k: np.asarray(v) for k, v in inputs.items()})
    nc = bacc.Bacc("TRN2", target_bir_lowering=False, num_devices=1)
    a = {k: nc.dram_tensor(f"in_{k}", v.shape, mybir.dt.from_np(v.dtype), kind="ExternalInput").ap() for k, v in arrays.items()}
    a["out"] = nc.dram_tensor("out", (TOK, D), F32, kind="ExternalOutput").ap()
    build_adaln_ffn(nc, a)
    r = run_bass_kernel_spmd(nc, [{f"in_{k}": v for k, v in arrays.items()}], core_ids=[0])
    return r.results[0]["out"].reshape(NB, CH, D)
```

```python
import concourse.bass as bass
from concourse import mybir
from contextlib import ExitStack

F32 = mybir.dt.float32
F32R = mybir.dt.float32r
BF16 = mybir.dt.bfloat16
I32 = mybir.dt.int32
U32 = mybir.dt.uint32
ALU = mybir.AluOpType
ACT = mybir.ActivationFunctionType
AX = mybir.AxisListType

P = 128
NB, CH, D = 32, 32, 512
TOK = NB * CH
NT = TOK // P
NPT = P // CH
R = D // P
TAPS = 9
QW = P + 2
OCT = 8
IN8, HID8, OUT8 = D // OCT, 170, D // OCT
OB = P // OCT
HC = -(-HID8 // OB)
HALF = TOK // 2
TPH = NT // 2
BW = HC * IN8
KC = 8
E = 32
DC = D // P
U = 8
NW = 2 * U
EARLY, MIDDLE = 3, 12
LAG = 5
XU = 2
G0 = E // U - 1
CHUNKS = TOK // P
XMAX = 16
PADROW = 1 << 20

C_ID, C_IO, C_MK, C_TRI, C_THR, C_ONE = 0, 128, 160, 164, 196, 204
CF_W = C_ONE + P
B_UP, B_ONE = 0, P
CB_W = 2 * P


def build_adaln_ffn(nc, a):
    ctx = ExitStack()
    with ctx:
        def dram(name, shape, dt):
            return nc.dram_tensor(name, shape, dt, kind="Internal").ap()

        y_tab = dram("y_tab", (TOK, D), F32)
        slots = dram("slots", ((CHUNKS + 1) * P * E, 4), I32)
        slots_v = slots.rearrange("(c p e) w -> c p e w", p=P, e=E)

        cur = [-(-nc.sbuf_base // 32) * 32]

        def region(size):
            at = cur[0]
            cur[0] += -(-size // 32) * 32
            assert cur[0] <= nc.sbuf_usable_end, (cur[0], nc.sbuf_usable_end)
            return at

        def put(name, shape, dt, at):
            return nc.alloc_sbuf_tensor_at(name, shape, dt, offset=at)

        def own(name, shape, dt):
            n = 4 if dt != BF16 else 2
            for s in shape[1:]:
                n *= s
            return put(name, shape, dt, region(n))

        class Cursor:

            def __init__(self, at, size):
                self.at, self.end = at, at + size

            def put(self, name, shape, dt):
                n = 4 if dt != BF16 else 2
                for s in shape[1:]:
                    n *= s
                t = put(name, shape, dt, self.at)
                self.at += -(-n // 32) * 32
                assert self.at <= self.end, name
                return t

        MB = R * HC * P * 4
        YB = R * TOK * 4
        r_w = region(EARLY * DC * D * 4)
        r_m = region(2 * MB)
        mg = put("mg", [P, R, HC, P], F32R, r_m)
        mu = put("mu", [P, R, HC, P], F32R, r_m + MB)
        r_y = region(2 * YB)
        y0hi = put("y0hi", [P, R, TOK], F32R, r_y)
        y0lo = put("y0lo", [P, R, TOK], F32R, r_y + YB)
        r_h = region(2 * HC * HALF * 4)
        hhi = put("hhi", [P, HC, HALF], F32R, r_h)
        hlo = put("hlo", [P, HC, HALF], F32R, r_h + HC * HALF * 4)
        md = own("md", [P, HC, D], F32R)
        acc = own("acc", [P, NT, D], F32)
        r_t = region(4 * D * 4)
        stmp = put("stmp", [P, 2, D], F32, r_t)
        htmp = put("htmp", [P, 2, D], F32, r_t + 2 * D * 4)
        r_yr = region(2 * D * 4)
        yv = put("yv", [P, 2, D], F32, r_yr)
        yT = own("yT", [P, DC, P], F32)
        su = Cursor(r_h, 2 * HC * HALF * 4)
        xp = su.put("xp", [P, NB, QW], F32)
        base = su.put("base", [P, 3, BW], F32)
        wc = su.put("wc", [P, 3, P], F32)
        cb = su.put("cb", [P, NB, CH], F32)
        diag = su.put("diag", [NB, NB, CH], F32)
        sel = su.put("sel", [NB, NT, P], F32)
        perm = su.put("perm", [P, OCT, P], BF16)
        wrep = su.put("wrep", [P, CH, KC], F32)
        prod = su.put("prod", [P, CH, KC], F32)
        w0s = su.put("w0s", [P, P], F32)
        w1s = su.put("w1s", [P, P], F32)
        cond, h1, h2 = (su.put(n, [P, NB], F32) for n in ("cond", "h1", "h2"))
        cwt, aggt = (su.put(n, [P, CH], F32) for n in ("cwt", "aggt"))
        asum = su.put("asum", [P, 3], F32)
        w2s, bkr = (su.put(n, [P, KC], F32) for n in ("w2s", "bkr"))
        tern = put("tern", [P, 3, BW], BF16, r_t)
        low = put("low", [P, BW], F32, r_t + 3 * BW * 2)
        convt = put("convt", [P, 2, R, P], F32, r_yr)
        ex = Cursor(r_w, EARLY * DC * D * 4 + 2 * MB + 2 * YB + 2 * HC * HALF * 4 + HC * D * 4)
        wbuf = [ex.put(f"wbuf{i}", [P, DC, D], F32) for i in range(NW)]
        yg = [ex.put(f"yg{i}", [P, D], F32) for i in range(U)]
        xT = [ex.put(f"xT{i}", [P, DC, P], F32) for i in range(2)]
        res = [ex.put(f"res{i}", [P, D], F32) for i in range(U)]
        cf = own("cf", [P, CF_W], F32)
        cbf = own("cbf", [P, CB_W], BF16)
        eb = own("eb", [E, D], F32)
        bd = own("bd", [P, NT, P], F32)
        gwt = own("gwt", [P, DC, E], F32)
        rec = own("rec", [P, NT, 2, 4], I32)
        rect = own("rect", [P, U, 4], I32)
        amat = own("amat", [P, NT, E], BF16)
        b01 = own("b01", [P, 2], F32)
        rows = own("rows", [1, CH + KC], F32)
        att = own("att", [NB, KC], F32)
        sm = own("sm", [NB, 4], F32)
        attx = own("attx", [P, NT, KC], F32)
        aggb = own("aggb", [P, NT], F32)
        wsc = own("wsc", [P, 3], F32)
        thr = own("thr", [P, 3], F32)
        nthr = own("nthr", [P, 3], F32)
        sud = own("sud", [P, 1], F32)
        lg = own("lg", [P, E], F32)
        mx = own("mx", [P, 8], F32)
        ix = own("ix", [P, 8], U32)
        oh = own("oh", [P, 2, E], F32)
        gap = own("gap", [P, 1], F32)
        th = own("th", [P, 1], F32)
        comb = own("comb", [P, E], F32)
        junk = own("junk", [P, E], F32)
        sidf = own("sidf", [P, 2], F32)
        sid = own("sid", [P, NT, 2], I32)
        combT = own("combT", [E, P], F32)
        cnt = own("cnt", [E, 1], F32)
        more = own("more", [E, 1], F32)
        incl = own("incl", [E, 1], F32)
        before = own("before", [E, XMAX], F32)
        lst = own("lst", [1, 2 * XMAX + 1 + XMAX], F32)
        todo = own("todo", [1, 2 * XMAX + 1], I32)

        bank = [ctx.enter_context(nc.psum_tensor(f"bank{i}", [P, 512], F32)) for i in range(8)]
        CONV = bank[0:2]
        CBB = bank[2:4]
        PG, PU = bank[2:4], bank[5:7]
        PD = (bank[4], bank[7])
        G, UU, DN = bank[0:2], bank[2:4], bank[5:7]
        BY, BT = bank[4], bank[7]
        XT, RS = bank[0:2], bank[2:4]

        def LG(j):
            return DN[0] if j == TPH - 1 else G[0]

        def PS(j):
            return DN[0] if j in (TPH - 2, TPH - 1) else UU[0]


        def sem(name):
            return ctx.enter_context(nc.semaphore(name))

        consts_in, conds_in, base_in, rest_in = (sem(s) for s in ("consts_in", "conds_in", "base_in", "rest_in"))
        xp_in = [sem(f"xp_in{g}") for g in range(NT)]
        acc_in = sem("acc_in")
        pads_in = sem("pads_in")
        w_in = [sem(f"w_in{b}") for b in range(NW)]
        dve_chain, act_chain = sem("dve_chain"), sem("act_chain")
        ctx_mm, diag_done, cb_mm, cb_done = (sem(s) for s in ("ctx_mm", "diag_done", "cb_mm", "cb_done"))
        h1_mm, h1_done, h2_mm, h2_done = (sem(s) for s in ("h1_mm", "h1_done", "h2_mm", "h2_done"))
        att_mm, att_max, att_exp, att_done = (sem(s) for s in ("att_mm", "att_max", "att_exp", "att_done"))
        attx_mm, attx_done, bd_done = (sem(s) for s in ("attx_mm", "attx_done", "bd_done"))
        asum_done, scale_mm, tern_done = (sem(s) for s in ("asum_done", "scale_mm", "tern_done"))
        pg_mm, pg_done, pu_mm, pu_done, pd_mm, pd_done = (sem(s) for s in ("pg_mm", "pg_done", "pu_mm", "pu_done", "pd_mm", "pd_done"))
        conv_mm, convt_done, y0hi_done, y0lo_done = (sem(s) for s in ("conv_mm", "convt_done", "y0hi_done", "y0lo_done"))
        g_mm, u_mm, silu_done, h_done, hhi_done, hlo_done = (sem(s) for s in ("g_mm", "u_mm", "silu_done", "h_done", "hhi_done", "hlo_done"))
        d_mm, acc_done = sem("d_mm"), sem("acc_done")
        y_mm, y_done, yt_mm, yt_done, lg_mm = (sem(s) for s in ("y_mm", "y_done", "yt_mm", "yt_done", "lg_mm"))
        y_stored = [sem(f"y_stored{i}") for i in range(2)]
        gap_done, th_done, choice_done, pos_mm, slots_done, combt_done, eb_mm, acc2_done = (
            sem(s) for s in ("gap_done", "th_done", "choice_done", "pos_mm", "slots_done", "combt_done", "eb_mm", "acc2_done"))
        recs_out = sem("recs_out")
        cnt_mm, more_done, incl_mm, before_done, list_mm, todo_done = (
            sem(s) for s in ("cnt_mm", "more_done", "incl_mm", "before_done", "list_mm", "todo_done"))
        rec_in = [sem(f"rec_in{b}") for b in range(U)]
        yg_in = [sem(f"yg_in{b}") for b in range(U)]
        res_out = sem("res_out")
        yg_zero, pool_steps, sp_steps = sem("yg_zero"), sem("pool_steps"), sem("sp_steps")
        xt_mm, xt_done, r_mm, res_done = (sem(s) for s in ("xt_mm", "xt_done", "r_mm", "res_done"))
        out_base = sem("out_base")

        ident = cf[:, C_ID:C_ID + P]
        iota = cf[:, C_IO:C_IO + E]
        bmask = cf[:, C_MK:C_MK + NPT]
        ones = cf[:, C_ONE:C_ONE + P]
        NCONST, NCOND, NREST = 5, 11, 5

        block = ctx.enter_context(nc.Block())

        def down_parts(g):
            return () if g < 2 else (g - 2,) if g < NT - 1 else range(NT - 3, OCT)

        @block.sync
        def _(sp):
            sp.dma_start(cond[:], a["condT"]).then_inc(conds_in, 16)
            sp.dma_start(cwt[:], a["cwT"]).then_inc(conds_in, 16)
            sp.dma_start(rows[:], a["rows"]).then_inc(conds_in, 16)
            sp.dma_start(cf[:], a["cf"]).then_inc(consts_in, 16)
            sp.dma_start(xp[:, 0:NPT], a["xp"][:, 0:NPT]).then_inc(xp_in[0], 16)
            sp.dma_start(base[:], a["base"]).then_inc(base_in, 16)
            for g in range(1, NT):
                sp.dma_start(xp[:, NPT * g:NPT * (g + 1)], a["xp"][:, NPT * g:NPT * (g + 1)]).then_inc(xp_in[g], 16)
            sp.dma_start(acc[:], a["x"].rearrange("(j p) d -> p j d", p=P)).then_inc(acc_in, 16)
            sp.dma_start(slots.rearrange("(c p e) w -> p c (e w)", p=P, e=E),
                         a["pads"].unsqueeze(1).to_broadcast([P, CHUNKS + 1, 4 * E])).then_inc(pads_in, 16)

            def load_w(e, b):
                for h_ in range(2):
                    sp.dma_start(wbuf[b][:, 2 * h_:2 * h_ + 2],
                                 a["w"][bass.ds(e, 1), :, 2 * h_:2 * h_ + 2].rearrange("a p c d -> p (a c) d")).then_inc(w_in[b], 16)

            def load_rec(chunk, e, b):
                sp.dma_start(rect[:, b], slots_v[bass.ds(chunk, 1), :, bass.ds(e, 1), :].rearrange("c p e w -> (c p) (e w)")).then_inc(rec_in[b], 16)

            for t in range(EARLY):
                load_w(t, t)

            def store_y(j):
                sp.wait_ge(y_done, j + 1)
                sp.dma_start(y_tab[P * j:P * (j + 1)], yv[:, j % 2]).then_inc(y_stored[j % 2], 16)

            def store_base(j):
                sp.wait_ge(acc2_done, j + 1)
                sp.dma_start(a["out"][P * j:P * (j + 1)], acc[:, j]).then_inc(out_base, 16)

            for j in range(NT):
                if j == TPH:
                    sp.wait_ge(u_mm, 2 * HC)
                    sp.wait_ge(g_mm, 2 * HC)
                if j >= TPH:
                    for t in range(EARLY, MIDDLE):
                        if (t - EARLY) * TPH // (MIDDLE - EARLY) == j - TPH:
                            load_w(t, t)
                store_y(j)
                if j % TPH >= 2:
                    store_base(j - 2)
                if j % TPH == TPH - 1:
                    if j == NT - 1:
                        sp.wait_ge(d_mm, NT)
                        for t in range(MIDDLE, NW):
                            load_w(t, t)
                    store_base(j - 1)
                    store_base(j)
            sp.dma_start(a["out"][TOK:TOK + P], acc[:, 0]).then_inc(out_base, 16)

            sp.wait_ge(recs_out, 2 * NT * 16)
            for t in range(U):
                load_rec(0, t, t)
            for u in range(U):
                sp.wait_ge(res_out, 16 * (u + 1))
                load_rec(0, U + u, u)
            with sp.Fori(1, G0) as g:
                for u in range(U):
                    sp.wait_ge(r_mm, g * U + (u + 1))
                    load_w(g * U + (U + u), U + u)
                    sp.wait_ge(res_out, g * (16 * U) + 16 * (u + 1))
                    load_rec(0, g * U + (U + u), u)

            sp.wait_ge(todo_done, 1)
            bodies = sp.value_load(todo[0:1, 2 * XMAX:2 * XMAX + 1], min_val=0, max_val=XMAX // XU - 1)
            for u in range(XU):
                e = sp.value_load(todo[0:1, u:u + 1], min_val=0, max_val=E - 1)
                c = sp.value_load(todo[0:1, XMAX + u:XMAX + u + 1], min_val=0, max_val=CHUNKS)
                sp.wait_ge(r_mm, E + u - U + 1)
                load_w(e, U + u)
                sp.wait_ge(res_out, 16 * (E + u - U + 1))
                load_rec(c, e, u)
            with sp.If(bodies > 0):
                with sp.Fori(1, bodies + 1) as g:
                    for u in range(XU):
                        e = sp.value_load(todo[0:1, bass.ds(g * XU + u, 1)], min_val=0, max_val=E - 1)
                        c = sp.value_load(todo[0:1, bass.ds(g * XU + (u + XMAX), 1)], min_val=0, max_val=CHUNKS)
                        sp.wait_ge(r_mm, g * XU + (E + u - XU + 1))
                        load_w(e, U + u)
                        sp.wait_ge(res_out, g * (16 * XU) + 16 * (E + u - XU + 1))
                        load_rec(c, e, u)
            sp.wait_ge(res_out, bodies * (16 * XU) + 16 * (E + XU))
            sp.sem_inc(sp_steps, 1)
            sp.wait_ge(out_base, 16 * (NT + 1))

        @block.gpsimd
        def _(pool):
            for g in range(NT):
                pool.wait_ge(y0hi_done, g + 1)
                nc.gpsimd.tensor_tensor(y0lo[:, :, P * g:P * (g + 1)], convt[:, g % 2], y0hi[:, :, P * g:P * (g + 1)].bitcast(F32), ALU.subtract).then_inc(y0lo_done, 1)
            pool.wait_ge(pads_in, 16)
            pool.wait_ge(rest_in, NREST * 16)
            for j in range(NT):
                pool.wait_ge(slots_done, j + 1)
                for k in range(2):
                    pool.indirect_dma_start(out=slots, out_offset=bass.IndirectOffsetOnAxis(ap=sid[:, j, k:k + 1], axis=0),
                                            in_=rec[:, j, k], in_offset=None).then_inc(recs_out, 16)
            pool.wait_ge(d_mm, NT)
            for b in range(U):
                nc.gpsimd.memset(yg[b][:], 0.0).then_inc(yg_zero, 1)
            pool.wait_ge(yg_zero, U)
            for i in range(2):
                pool.wait_ge(y_stored[i], NT // 2 * 16)

            last_token, last_row = pool.to_reg(TOK - 1), pool.to_reg(TOK + P - 1)

            def gather(n, b, used=None):
                pool.wait_ge(rec_in[b], n * 16)
                if used is not None:
                    pool.wait_ge(xt_mm, used)
                pool.sem_inc(pool_steps, 1)
                pool.indirect_dma_start(out=yg[b][:], out_offset=None, in_=y_tab,
                                        in_offset=bass.IndirectOffsetOnAxis(ap=rect[:, b, 0:1].bitcast(U32), axis=0),
                                        bounds_check=last_token, oob_is_err=False).then_inc(yg_in[b], 16)

            def scatter(t, b):
                pool.wait_ge(res_done, t + 1)
                if not (isinstance(t, int) and t == 0):
                    pool.wait_ge(res_out, t * 16)
                pool.sem_inc(pool_steps, 1)
                pool.indirect_dma_start(out=a["out"], out_offset=bass.IndirectOffsetOnAxis(ap=rect[:, b, 1:2].bitcast(U32), axis=0),
                                        in_=res[b][:], in_offset=None, compute_op=ALU.add,
                                        bounds_check=last_row).then_inc(res_out, 16)

            for t in range(U):
                gather(1, t)
                if t == LAG:
                    pool.wait_ge(out_base, 16 * (NT + 1))
                if t >= LAG:
                    scatter(t - LAG, t - LAG)
            with pool.Fori(0, G0) as g:
                for u in range(U):
                    gather(g + 2, u, g * U + (u + 1))
                    scatter(g * U + (U + u - LAG), (u - LAG) % U)
            for u in range(XU):
                gather(G0 + 2, u, E + u - U + 1)
                scatter(E + u - LAG, (u - LAG) % U)
            for t in range(E + XU - LAG, E + XU):
                scatter(t, t % U)
            pool.wait_ge(todo_done, 1)
            bodies = pool.value_load(todo[0:1, 2 * XMAX:2 * XMAX + 1], min_val=0, max_val=XMAX // XU - 1)
            with pool.If(bodies > 0):
                with pool.Fori(1, bodies + 1) as g:
                    for u in range(XU):
                        gather(g + (G0 + 2), u, g * XU + (E + u - XU + 1))
                    for u in range(XU):
                        scatter(g * XU + (E + u), u)

        @block.scalar
        def _(act):
            chain = [0]

            def link(ins):
                chain[0] += 1
                ins.then_inc(act_chain, 1)
                act.wait_ge(act_chain, chain[0])

            for t, k in ((b01, "b01"), (w0s, "w0"), (w1s, "w1"), (w2s, "w2"), (sel, "sel"), (wrep, "wrep"), (bkr, "bkr"), (gwt, "gwT")):
                act.dma_start(t[:], a[k]).then_inc(conds_in, 16)
            for t, k in ((perm, "perm"), (cbf, "cb")):
                act.dma_start(t[:], a[k].bitcast(BF16)).then_inc(consts_in, 16)
            for t, k in ((wc, "wc"), (eb, "eb")):
                act.dma_start(t[:], a[k]).then_inc(consts_in, 16)
            act.dma_start(rec[:], a["rec"]).then_inc(rest_in, 16 * NREST)
            for hm, bcol, h, hd in ((h1_mm, 0, h1, h1_done), (h2_mm, 1, h2, h2_done)):
                act.wait_ge(hm, 1)
                nc.scalar.activation(h[:], BY[:, NB * bcol:NB * (bcol + 1)], ACT.Gelu, bias=b01[:, bcol:bcol + 1]).then_inc(hd, 1)
                if bcol == 0:
                    act.wait_ge(base_in, 16)
                    for m in range(3):
                        if m:
                            act.wait_ge(asum_done, m)
                        nc.scalar.activation(low[:], base[:, m], ACT.Abs, accum_out=asum[:, m:m + 1]).then_inc(asum_done, 1)
                    act.wait_ge(cb_mm, 1)
                    for h_ in range(2):
                        nc.scalar.activation(cb[:].rearrange("p n c -> p (n c)")[:, 512 * h_:512 * (h_ + 1)], CBB[h_][:], ACT.Copy).then_inc(cb_done, 1)

            act.wait_ge(att_max, 1)
            nc.scalar.activation(att[:], BY[0:NB, 64:64 + KC], ACT.Exp, bias=sm[:, 1:2], accum_out=sm[:, 2:3]).then_inc(att_exp, 1)

            def conv_hi(g):
                act.wait_ge(convt_done, g + 1)
                nc.scalar.activation(y0hi[:, :, P * g:P * (g + 1)], convt[:, g % 2], ACT.Copy).then_inc(y0hi_done, 1)

            def gate_table(k):
                act.wait_ge(pg_mm, k + 1)
                for h_ in range(2):
                    v = nc.scalar.activation(mg[:, 2 * h_:2 * h_ + 2, :, OB * k:OB * (k + 1)],
                                             PG[h_][:, 0:BW // 2].rearrange("p (r c o) -> p r c o", r=2, o=OB), ACT.Copy)
                v.then_inc(pg_done, 1)

            def down_table(k):
                act.wait_ge(pd_mm, k + 1)
                for h_, (c0, c1) in enumerate(((0, 6), (6, HC))):
                    v = nc.scalar.activation(md[:, c0:c1, OUT8 * k:OUT8 * (k + 1)],
                                             PD[h_][:, 0:(c1 - c0) * OUT8].rearrange("p (c o) -> p c o", o=OUT8), ACT.Copy)
                v.then_inc(pd_done, 1)

            for g in range(NT):
                conv_hi(g)
                gate_table(g)
                for k in down_parts(g):
                    down_table(k)
                if g == 1:
                    act.wait_ge(attx_mm, 1)
                    nc.scalar.activation(attx[:].rearrange("p g k -> p (g k)"), BT[:, 64:64 + NT * KC], ACT.Copy).then_inc(attx_done, 1)

            def silu(n):
                act.wait_ge(g_mm, n + 1)
                if n >= 2:
                    act.wait_ge(h_done, n - 1)
                nc.scalar.activation(stmp[:, n % 2], G[n % 2][:], ACT.Silu, scale=wsc[:, 0:1]).then_inc(silu_done, 1)

            def hid_hi(n):
                act.wait_ge(h_done, n + 1)
                nc.scalar.activation(hhi[:, n % HC], htmp[:, n % 2], ACT.Copy).then_inc(hhi_done, 1)

            def y_evac(j):
                act.wait_ge(y_mm, j + 1)
                if j == 0:
                    act.wait_ge(y0lo_done, NT)
                if j >= 2:
                    act.wait_ge(y_stored[j % 2], j // 2 * 16)
                    act.wait_ge(yt_mm, j - 1)
                nc.scalar.activation(yv[:, j % 2], BY[:], ACT.Identity, bias=aggb[:, j:j + 1]).then_inc(y_done, 1)

            def yt_evac(j):
                act.wait_ge(yt_mm, j + 1)
                if j >= 1:
                    act.wait_ge(lg_mm, j)
                nc.scalar.activation(yT[:].rearrange("p c t -> p (c t)"), BT[:], ACT.Copy).then_inc(yt_done, 1)

            def weight_tanh(j):
                act.wait_ge(gap_done, j + 1)
                nc.scalar.activation(th[:], gap[:], ACT.Tanh, scale=0.5).then_inc(th_done, 1)

            act.wait_ge(tern_done, 3)
            for half in range(2):
                for c in range(HC):
                    n = half * HC + c
                    silu(n)
                    if c >= 1:
                        hid_hi(n - 1)
                    if half == 1:
                        if c == 0:
                            y_evac(TPH - 1)
                        if c == 3:
                            yt_evac(TPH - 1)
                        if c == 6:
                            weight_tanh(TPH - 1)
                hid_hi(half * HC + HC - 1)
                for t in range(1, TPH):
                    j = half * TPH + t
                    y_evac(j - 1)
                    if t >= 2:
                        weight_tanh(j - 2)
                    yt_evac(j - 1)
                if half == 0:
                    weight_tanh(TPH - 2)
            y_evac(NT - 1)
            weight_tanh(NT - 2)
            yt_evac(NT - 1)
            weight_tanh(NT - 1)

            def evac(t, n, b, scattered=None):
                act.wait_ge(rec_in[b], n * 16)
                act.wait_ge(r_mm, t + 1)
                if scattered is not None:
                    act.wait_ge(res_out, scattered)
                nc.scalar.activation(res[b][:], RS[b % 2][:], ACT.Copy, scale=rect[:, b, 2:3].bitcast(F32)).then_inc(res_done, 1)

            for t in range(U):
                evac(t, 1, t)
            with act.Fori(0, G0) as g:
                for u in range(U):
                    evac(g * U + (U + u), g + 2, u, g * (16 * U) + 16 * (u + 1))
            for u in range(XU):
                evac(E + u, G0 + 2, u, 16 * (E + u - U + 1))
            act.wait_ge(todo_done, 1)
            bodies = act.value_load(todo[0:1, 2 * XMAX:2 * XMAX + 1], min_val=0, max_val=XMAX // XU - 1)
            with act.If(bodies > 0):
                with act.Fori(1, bodies + 1) as g:
                    for u in range(XU):
                        evac(g * XU + (E + u), g + (G0 + 2), u, g * (16 * XU) + 16 * (E + u - XU + 1))

        @block.vector
        def _(dve):
            chain = [0]

            def link(ins):
                chain[0] += 1
                ins.then_inc(dve_chain, 1)
                dve.wait_ge(dve_chain, chain[0])

            dve.wait_ge(consts_in, NCONST * 16)
            dve.wait_ge(ctx_mm, 1)
            nc.vector.tensor_tensor(diag[:], BT[0:NB, 0:CH].unsqueeze(1).to_broadcast([NB, NB, CH]),
                                    ident[0:NB, 0:NB].unsqueeze(2).to_broadcast([NB, NB, CH]), ALU.mult).then_inc(diag_done, 1)
            dve.wait_ge(scale_mm, 1)
            nc.vector.tensor_scalar(wsc[:], BT[:, 32:35], 1.0 / (OCT * HID8 * IN8), None, ALU.mult).then_inc(dve_chain, 1)
            chain[0] += 1
            dve.wait_ge(dve_chain, chain[0])
            nc.vector.tensor_scalar(thr[:], wsc[:], 0.5, None, ALU.mult).then_inc(dve_chain, 1)
            nc.vector.tensor_scalar(nthr[:], wsc[:], -0.5, None, ALU.mult).then_inc(dve_chain, 1)
            nc.vector.tensor_tensor(sud[:], wsc[:, 1:2], wsc[:, 2:3], ALU.mult).then_inc(dve_chain, 1)
            chain[0] += 3
            dve.wait_ge(dve_chain, chain[0])

            def quantize(m):
                link(nc.vector.tensor_scalar(low[:], base[:, m], nthr[:, m:m + 1], None, ALU.is_lt))
                nc.vector.scalar_tensor_tensor(tern[:, m], base[:, m], thr[:, m:m + 1], low[:], ALU.is_gt, ALU.subtract).then_inc(tern_done, 1)
                dve.wait_ge(tern_done, m + 1)

            def conv_evac(g):
                dve.wait_ge(conv_mm, g + 1)
                if g == 0:
                    dve.wait_ge(cb_done, 2)
                if g >= 2:
                    dve.wait_ge(y0hi_done, g - 1)
                    dve.wait_ge(y0lo_done, g - 1)
                nc.vector.tensor_tensor(convt[:, g % 2].rearrange("p r (n c) -> p r n c", c=CH),
                                        CONV[g % 2][:].rearrange("p (n r c) -> p r n c", n=NPT, c=CH),
                                        cb[:, NPT * g:NPT * (g + 1)].unsqueeze(1).to_broadcast([P, R, NPT, CH]), ALU.add).then_inc(convt_done, 1)

            def up_table(k):
                dve.wait_ge(pu_mm, k + 1)
                for h_ in range(2):
                    v = nc.vector.tensor_copy(mu[:, 2 * h_:2 * h_ + 2, :, OB * k:OB * (k + 1)],
                                              PU[h_][:, 0:BW // 2].rearrange("p (r c o) -> p r c o", r=2, o=OB))
                v.then_inc(pu_done, 1)

            quantize(0)
            quantize(1)
            for g in range(NT):
                conv_evac(g)
                up_table(g)
                if g == 0:
                    quantize(2)
                    dve.wait_ge(att_mm, 1)
                    link(nc.vector.reduce_max(sm[:, 0:1], BY[0:NB, 64:64 + KC], axis=AX.X))
                    nc.vector.tensor_scalar(sm[:, 1:2], sm[:, 0:1], -1.0, None, ALU.mult).then_inc(att_max, 1)
                    dve.wait_ge(att_exp, 1)
                    link(nc.vector.reciprocal(sm[:, 3:4], sm[:, 2:3]))
                    nc.vector.tensor_scalar(att[:], att[:], sm[:, 3:4], None, ALU.mult).then_inc(att_done, 1)
                if g == 1:
                    dve.wait_ge(attx_done, 1)
                    link(nc.vector.tensor_tensor(prod[:, 0:NT, :], attx[:], bkr[:].unsqueeze(1).to_broadcast([P, NT, KC]), ALU.mult))
                    link(nc.vector.tensor_reduce(aggb[:], prod[:, 0:NT, :], AX.X, ALU.add))
                if g >= 1:
                    for t in ((g - 1, NT - 1) if g == NT - 1 else (g - 1,)):
                        link(nc.vector.tensor_tensor(prod[:], wrep[:], attx[:, t].unsqueeze(1).to_broadcast([P, CH, KC]), ALU.mult))
                        link(nc.vector.tensor_reduce(aggt[:], prod[:], AX.X, ALU.add))
                        link(nc.vector.tensor_tensor(bd[:, t].rearrange("p (b o) -> p b o", b=NPT),
                                                     aggt[:].unsqueeze(1).to_broadcast([P, NPT, CH]),
                                                     bmask.unsqueeze(2).to_broadcast([P, NPT, CH]), ALU.mult))

            def hidden(n):
                dve.wait_ge(silu_done, n + 1)
                dve.wait_ge(u_mm, n + 1)
                if n >= 2:
                    dve.wait_ge(hhi_done, n - 1)
                    dve.wait_ge(hlo_done, n - 1)
                nc.vector.tensor_tensor(htmp[:, n % 2], UU[n % 2][:], stmp[:, n % 2], ALU.mult).then_inc(h_done, 1)

            def hid_lo(n):
                dve.wait_ge(hhi_done, n + 1)
                nc.vector.tensor_tensor(hlo[:, n % HC], htmp[:, n % 2], hhi[:, n % HC].bitcast(F32), ALU.subtract).then_inc(hlo_done, 1)

            def acc_evac(j):
                if j == 0:
                    dve.wait_ge(acc_in, 16)
                dve.wait_ge(d_mm, j + 1)
                nc.vector.scalar_tensor_tensor(acc[:, j], DN[j % 2][:], sud[:, 0:1], acc[:, j], ALU.mult, ALU.add).then_inc(acc_done, 1)

            def choose(j):
                dve.wait_ge(lg_mm, j + 1)
                link(nc.vector.max(mx[:], LG(j)[:, 0:E]))
                nc.vector.tensor_tensor(gap[:], mx[:, 0:1], mx[:, 1:2], ALU.subtract).then_inc(gap_done, 1)
                link(nc.vector.max_index(ix[:], mx[:], LG(j)[:, 0:E]))
                for k in range(2):
                    link(nc.vector.tensor_scalar(oh[:, k], iota, ix[:, k:k + 1], None, ALU.is_equal))
                link(nc.vector.tensor_tensor(amat[:, j], oh[:, 0], oh[:, 1], ALU.add))

            def weigh(j):
                dve.wait_ge(th_done, j + 1)
                for k, s in ((0, 0.5), (1, -0.5)):
                    link(nc.vector.tensor_scalar(rec[:, j, k, 2:3].bitcast(F32), th[:], s, 0.5, ALU.mult, ALU.add))
                link(nc.vector.tensor_scalar(comb[:], oh[:, 0], rec[:, j, 0, 2:3].bitcast(F32), None, ALU.mult))
                nc.vector.scalar_tensor_tensor(comb[:], oh[:, 1], rec[:, j, 1, 2:3].bitcast(F32), comb[:], ALU.mult, ALU.add).then_inc(choice_done, 1)

            def place(j):
                dve.wait_ge(pos_mm, j + 1)
                nc.vector.tensor_copy(combT[:], PS(j)[0:E, 64:64 + P]).then_inc(combt_done, 1)
                link(nc.vector.scalar_tensor_tensor(lg[:], PS(j)[:, E:2 * E], float(E), iota, ALU.mult, ALU.add))
                for k in range(2):
                    link(nc.vector.scalar_tensor_tensor(junk[:], iota, ix[:, k:k + 1], lg[:], ALU.is_equal, ALU.mult, accum_out=sidf[:, k:k + 1]))
                nc.vector.tensor_copy(sid[:, j], sidf[:]).then_inc(slots_done, 1)
                dve.wait_ge(slots_done, j + 1)

            def add_bias(j):
                dve.wait_ge(eb_mm, j + 1)
                nc.vector.tensor_tensor(acc[:, j], acc[:, j], BT[:], ALU.add).then_inc(acc2_done, 1)

            dve.wait_ge(rest_in, NREST * 16)
            for half in range(2):
                for c in range(HC):
                    n = half * HC + c
                    hidden(n)
                    if c >= 1:
                        hid_lo(n - 1)
                    if half == 1:
                        if c == 2:
                            place(TPH - 2)
                        if c == 3:
                            add_bias(TPH - 2)
                        if c == 5:
                            choose(TPH - 1)
                        if c == 6:
                            weigh(TPH - 1)
                        if c == 8:
                            place(TPH - 1)
                        if c == 10:
                            add_bias(TPH - 1)
                hid_lo(half * HC + HC - 1)
                for t in range(TPH):
                    j = half * TPH + t
                    if t >= 2:
                        choose(j - 2)
                        weigh(j - 2)
                        place(j - 2)
                        add_bias(j - 2)
                    acc_evac(j)
                if half == 0:
                    choose(TPH - 2)
                    weigh(TPH - 2)
            choose(NT - 2)
            weigh(NT - 2)
            place(NT - 2)
            choose(NT - 1)
            weigh(NT - 1)
            add_bias(NT - 2)
            place(NT - 1)
            add_bias(NT - 1)

            def xt_evac(i, u, first=False):
                dve.wait_ge(xt_mm, i + 1)
                if not first:
                    dve.wait_ge(r_mm, i - 1)
                nc.vector.tensor_copy(xT[u % 2][:].rearrange("p c t -> p (c t)"), XT[u % 2][:]).then_inc(xt_done, 1)

            xt_evac(0, 0, True)
            xt_evac(1, 1, True)
            dve.wait_ge(cnt_mm, 1)
            link(nc.vector.tensor_copy(cnt[:], BY[0:E, 0:1]))
            nc.vector.tensor_scalar(junk[0:E, 0:8], cf[0:E, C_THR:C_THR + 8], cnt[:, 0:1], 0.0, ALU.is_lt, ALU.add, accum_out=more[:]).then_inc(more_done, 1)
            dve.wait_ge(incl_mm, 1)
            link(nc.vector.tensor_copy(incl[:], BY[0:E, 0:1]))
            nc.vector.tensor_scalar(before[:], iota[0:E, 0:XMAX], incl[:, 0:1], None, ALU.is_ge).then_inc(before_done, 1)
            dve.wait_ge(list_mm, 1)
            ends = lst[:, 2 * XMAX + 1:]
            link(nc.vector.tensor_copy(lst[:, 0:2 * XMAX + 1], BY[0:1, 0:2 * XMAX + 1]))
            link(nc.vector.tensor_scalar(ends, lst[:, 0:XMAX], float(E), None, ALU.is_ge))
            link(nc.vector.tensor_tensor(lst[:, 0:XMAX], lst[:, 0:XMAX], ends, ALU.subtract))
            link(nc.vector.scalar_tensor_tensor(lst[:, XMAX:2 * XMAX], iota[0:1, 0:XMAX], 1.0, lst[:, XMAX:2 * XMAX], ALU.add, ALU.subtract))
            link(nc.vector.scalar_tensor_tensor(junk[0:1, 0:XMAX], ends, float(CHUNKS), lst[:, XMAX:2 * XMAX], ALU.mult, ALU.max))
            link(nc.vector.tensor_copy(lst[:, XMAX:2 * XMAX], junk[0:1, 0:XMAX]))
            link(nc.vector.tensor_scalar(junk[0:1, 0:XMAX // XU - 1], cf[0:1, C_IO + XU:C_IO + XMAX:XU], lst[:, 2 * XMAX:2 * XMAX + 1], 0.0, ALU.is_lt, ALU.add,
                                         accum_out=lg[0:1, 0:1]))
            nc.vector.tensor_copy(todo[:, 2 * XMAX:2 * XMAX + 1], lg[0:1, 0:1]).then_inc(dve_chain, 1)
            chain[0] += 1
            link(nc.vector.tensor_copy(todo[:, 0:2 * XMAX], lst[:, 0:2 * XMAX]))
            nc.vector.engine_nop().then_inc(todo_done, 1)
            for t in range(2, U):
                xt_evac(t, t)
            with dve.Fori(0, G0) as g:
                for u in range(U):
                    xt_evac(g * U + (U + u), u)
            for u in range(XU):
                xt_evac(E + u, u)
            bodies = dve.value_load(todo[0:1, 2 * XMAX:2 * XMAX + 1], min_val=0, max_val=XMAX // XU - 1)
            with dve.If(bodies > 0):
                with dve.Fori(1, bodies + 1) as g:
                    for u in range(XU):
                        xt_evac(g * XU + (E + u), u)

        @block.tensor
        def _(pe):
            mm = nc.tensor.matmul

            pe.wait_ge(conds_in, NCOND * 16)
            pe.wait_ge(consts_in, NCONST * 16)
            mm(BT[0:NB, 0:CH], cond[:], cwt[:], start=True, stop=False)
            mm(BT[0:NB, 0:CH], ones[0:1, 0:NB], rows[:, 0:CH], start=False, stop=True).then_inc(ctx_mm, 1)
            mm(BY[:, 0:NB], w0s[:], cond[:], start=True, stop=True).then_inc(h1_mm, 1)
            pe.wait_ge(diag_done, 1)
            for h_ in range(2):
                v = mm(CBB[h_][:], ones[0:NB, :], diag[:].rearrange("b n c -> b (n c)")[:, 512 * h_:512 * (h_ + 1)], start=True, stop=True)
            v.then_inc(cb_mm, 1)

            def conv(g):
                pe.wait_ge(xp_in[g], 16)
                if g >= 2:
                    pe.wait_ge(convt_done, g - 1)
                for b in range(NPT):
                    for s in range(3):
                        v = mm(CONV[g % 2][:, P * b:P * (b + 1)], xp[:, NPT * g + b, s:s + P], wc[:, s], start=(s == 0), stop=(s == 2))
                v.then_inc(conv_mm, 1)

            def table(k, m, banks, made, used):
                if k >= 1:
                    pe.wait_ge(used, k)
                cut = BW // 2 if m < 2 else 6 * OUT8
                for h_, (c0, c1) in enumerate(((0, cut), (cut, BW))):
                    v = mm(banks[h_][:, 0:c1 - c0], perm[:, k], tern[:, m, c0:c1], start=True, stop=True)
                v.then_inc(made, 1)

            pe.wait_ge(asum_done, 3)
            mm(BT[:, 32:35], ones, asum[:], start=True, stop=True).then_inc(scale_mm, 1)
            pe.wait_ge(h1_done, 1)
            mm(BY[:, NB:2 * NB], w1s[:], h1[:], start=True, stop=True).then_inc(h2_mm, 1)
            conv(0)
            pe.wait_ge(h2_done, 1)
            mm(BY[0:NB, 64:64 + KC], h2[:], w2s[:], start=True, stop=False)
            mm(BY[0:NB, 64:64 + KC], ones[0:1, 0:NB], rows[:, CH:CH + KC], start=False, stop=True).then_inc(att_mm, 1)
            pe.wait_ge(cb_done, 2)
            for g in range(NT):
                if g >= 1:
                    conv(g)
                if g == 0:
                    pe.wait_ge(tern_done, 2)
                table(g, 0, PG, pg_mm, pg_done)
                table(g, 1, PU, pu_mm, pu_done)
                if g == 1:
                    pe.wait_ge(att_done, 1)
                    for t in range(NT):
                        v = mm(BT[:, 64 + KC * t:64 + KC * (t + 1)], sel[:, t], att[:], start=True, stop=True)
                    v.then_inc(attx_mm, 1)
                if g == 2:
                    pe.wait_ge(attx_done, 1)
                    pe.wait_ge(tern_done, 3)
                for k in down_parts(g):
                    table(k, 2, PD, pd_mm, pd_done)
            pe.wait_ge(pg_done, OCT)
            pe.wait_ge(pu_done, OCT)

            def hidden(n, half):
                c = n % HC
                if n % HC == 0:
                    pe.wait_ge(y0hi_done, (half + 1) * TPH)
                    pe.wait_ge(y0lo_done, (half + 1) * TPH)
                for banks, tab, used, made in ((G, mg, silu_done, g_mm), (UU, mu, h_done, u_mm)):
                    if n >= 2:
                        pe.wait_ge(used, n - 1)
                    for r in range(R):
                        for part, y in enumerate((y0hi, y0lo)):
                            v = mm(banks[n % 2][:], tab[:, r, c], y[:, r, HALF * half:HALF * (half + 1)],
                                   start=(r == 0 and part == 0), stop=(r == R - 1 and part == 1))
                    v.then_inc(made, 1)

            issued = {"yt": 0, "bias": 0}

            def y(j):
                pe.wait_ge(acc_done, j + 1)
                if j >= 1:
                    pe.wait_ge(y_done, j)
                mm(BY[:], bd[:, j], acc[:, j], start=True, stop=True).then_inc(y_mm, 1)

            def bank_read():
                if issued["yt"]:
                    pe.wait_ge(yt_done, issued["yt"])
                if issued["bias"]:
                    pe.wait_ge(acc2_done, issued["bias"])

            def yt(j):
                pe.wait_ge(y_done, j + 1)
                bank_read()
                for c in range(DC):
                    v = nc.tensor.transpose(BT[:, P * c:P * (c + 1)], yv[:, j % 2, P * c:P * (c + 1)], ident)
                v.then_inc(yt_mm, 1)
                issued["yt"] += 1

            def logits(j):
                pe.wait_ge(yt_done, j + 1)
                if j >= 1:
                    pe.wait_ge(choice_done, j)
                if j == TPH - 1:
                    pe.wait_ge(slots_done, j)
                for c in range(DC):
                    v = mm(LG(j)[:, 0:E], yT[:, c], gwt[:, c], start=(c == 0), stop=(c == DC - 1))
                v.then_inc(lg_mm, 1)

            def positions(j):
                pe.wait_ge(choice_done, j + 1)
                if j >= 1:
                    pe.wait_ge(slots_done, j)
                for t in range(j):
                    mm(PS(j)[:, E:2 * E], cbf[:, B_ONE:B_ONE + P], amat[:, t], start=(t == 0), stop=False)
                mm(PS(j)[:, E:2 * E], cbf[:, B_UP:B_UP + P], amat[:, j], start=(j == 0), stop=True)
                nc.tensor.transpose(PS(j)[0:E, 64:64 + P], comb[:], ident).then_inc(pos_mm, 1)

            def bias(j):
                pe.wait_ge(combt_done, j + 1)
                bank_read()
                mm(BT[:], combT[:], eb[:], start=True, stop=True).then_inc(eb_mm, 1)
                issued["bias"] += 1

            L = TPH - 1
            beside_hidden = {0: (y, L), 1: (positions, L - 1), 2: (yt, L), 3: (bias, L - 1), 4: (logits, L), 7: (positions, L), 9: (bias, L)}

            def beside_down(j):
                t = j % TPH
                return {**({1: (y, j - 1), 4: (yt, j - 1), 8: (logits, j - 1)} if t >= 1 else {}),
                        **({6: (positions, j - 2), 10: (bias, j - 2)} if t >= 2 else {})}

            def down(j):
                half, t = divmod(j, TPH)
                if j >= 2:
                    pe.wait_ge(acc_done, j - 1)
                if j == TPH:
                    pe.wait_ge(slots_done, TPH)
                steps = beside_down(j)
                for c in range(HC):
                    if t == 0:
                        pe.wait_ge(hhi_done, half * HC + c + 1)
                        pe.wait_ge(hlo_done, half * HC + c + 1)
                    for part, h in enumerate((hhi, hlo)):
                        v = mm(DN[j % 2][:], h[:, c, P * t:P * (t + 1)], md[:, c], start=(c == 0 and part == 0), stop=(c == HC - 1 and part == 1))
                    if c == HC - 1:
                        v.then_inc(d_mm, 1)
                    if c in steps:
                        step, tile = steps[c]
                        step(tile)

            for half in range(2):
                for c in range(HC):
                    if half == 1 and c == 1:
                        pe.wait_ge(choice_done, TPH - 1)
                    hidden(half * HC + c, half)
                    if half == 1 and c in beside_hidden:
                        step, tile = beside_hidden[c]
                        step(tile)
                pe.wait_ge(pd_done, OCT)
                for t in range(TPH):
                    down(half * TPH + t)
            y(NT - 1)
            positions(NT - 2)
            yt(NT - 1)
            logits(NT - 1)
            bias(NT - 2)
            positions(NT - 1)
            bias(NT - 1)

            def transposes(t, n, b, first=False):
                pe.wait_ge(yg_in[b], n * 16)
                if not first:
                    pe.wait_ge(xt_done, t - 1)
                for c in range(DC):
                    v = nc.tensor.transpose(XT[b % 2][:, P * c:P * (c + 1)], yg[b][:, P * c:P * (c + 1)], ident)
                v.then_inc(xt_mm, 1)

            def product(t, n, b, first=False):
                pe.wait_ge(xt_done, t + 1)
                pe.wait_ge(w_in[b], n * 32)
                if not first:
                    pe.wait_ge(res_done, t - 1)
                for c in range(DC):
                    v = mm(RS[b % 2][:], xT[b % 2][:, c], wbuf[b][:, c], start=(c == 0), stop=(c == DC - 1))
                v.then_inc(r_mm, 1)

            transposes(0, 1, 0, True)
            for j in range(NT):
                v = mm(BY[0:E, 0:1], amat[:, j], cbf[:, B_ONE:B_ONE + 1], start=(j == 0), stop=(j == NT - 1))
            v.then_inc(cnt_mm, 1)
            transposes(1, 1, 1, True)
            product(0, 1, 0, True)
            pe.wait_ge(more_done, 1)
            mm(BY[0:E, 0:1], cf[0:E, C_TRI:C_TRI + E], more[:], start=True, stop=True).then_inc(incl_mm, 1)
            pe.wait_ge(before_done, 1)
            mm(BY[0:1, 0:XMAX], ones[0:E, 0:1], before[:], start=True, stop=True)
            mm(BY[0:1, XMAX:2 * XMAX], more[:], before[:], start=True, stop=True)
            mm(BY[0:1, 2 * XMAX:2 * XMAX + 1], more[:], ones[0:E, 0:1], start=True, stop=True).then_inc(list_mm, 1)
            for t in range(2, U):
                transposes(t, 1, t)
                product(t - 1, 1, t - 1, t - 1 < 2)
            transposes(U, 2, 0)
            product(U - 1, 1, U - 1)
            with pe.Fori(0, G0) as g:
                for u in range(U):
                    if u < U - 1:
                        transposes(g * U + (U + u + 1), g + 2, u + 1)
                    else:
                        transposes(g * U + (2 * U), g + 3, 0)
                    product(g * U + (U + u), g + 1, U + u)
            for u in range(XU):
                if u < XU - 1:
                    transposes(E + u + 1, G0 + 2, u + 1)
                product(E + u, G0 + 1, U + u)
            pe.wait_ge(todo_done, 1)
            bodies = pe.value_load(todo[0:1, 2 * XMAX:2 * XMAX + 1], min_val=0, max_val=XMAX // XU - 1)
            with pe.If(bodies > 0):
                with pe.Fori(1, bodies + 1) as g:
                    for u in range(XU):
                        transposes(g * XU + (E + u), g + (G0 + 2), u)
                    for u in range(XU):
                        product(g * XU + (E + u), g + (G0 + 1), U + u)


def layouts(i):
    import numpy as np

    f = np.float32
    x = i["x"]
    out = {}
    xp = np.zeros((R, CH, NB, QW), f)
    xp[:, :, :, 1:1 + P] = x.reshape(NB, CH, P, R).transpose(3, 1, 0, 2)
    out["xp"] = xp.reshape(P, NB, QW)
    out["x"] = x.reshape(TOK, D)
    cw = i["L0_cond_weight"]
    per = CH // 4
    wc = np.zeros((R, CH, 3, R, CH), f)
    for s in range(R):
        for d in range(3):
            for r in range(R):
                tap = 4 * (d - 1) + s - r + 4
                if 0 <= tap < TAPS:
                    for co in range(CH):
                        g0 = co // per * per
                        wc[s, g0:g0 + per, d, r, co] = cw[co, :, tap]
    out["wc"] = wc.reshape(P, 3, P)

    def hidden_pad(w, axis):
        shape = list(w.shape)
        shape[axis] = HC * OB
        p = np.zeros(shape, f)
        p[tuple(slice(0, n) for n in w.shape)] = w
        return p

    base = np.zeros((P, 3, BW), f)
    for m, k in enumerate(("L0_ffn_w_gate", "L0_ffn_w_up")):
        w = hidden_pad(i[k], 1).reshape(OCT, HC * OB, OB, R)
        base[:, m] = w.transpose(0, 2, 3, 1).reshape(P, BW)
    w = hidden_pad(i["L0_ffn_w_down"], 2).reshape(OCT, OUT8, HC, OB)
    base[:, 2] = w.transpose(0, 3, 2, 1).reshape(P, BW)
    out["base"] = base
    out["condT"] = i["cond_128"].T
    out["cwT"] = i["L0_cond_c_weight"].T
    out["rows"] = np.concatenate([i["fside_S_0"], i["L1_cond_b2"]])[None]
    out["b01"] = np.stack([i["L1_cond_b0"], i["L1_cond_b1"]], 1)
    out["w0"], out["w1"], out["w2"] = i["L1_cond_W0"], i["L1_cond_W1"], i["L1_cond_W2"]
    out["wrep"] = np.tile(i["L1_cond_weight"][..., 0].transpose(2, 1, 0), (NPT, 1, 1))
    out["bkr"] = np.tile(i["L1_cond_bias_k"].T, (NPT, 1))
    out["gwT"] = i["L1_ffn_gate_w"].T.reshape(DC, P, E).transpose(1, 0, 2)
    out["w"] = i["L1_ffn_expert_w"].reshape(E, D, DC, P).transpose(0, 3, 2, 1)
    out["eb"] = i["L1_ffn_expert_b"]

    def bf16_bits(v):
        return (np.ascontiguousarray(v).view(np.uint32) >> 16).astype(np.uint16)

    sel = np.zeros((NB, NT, P), f)
    for b in range(NB):
        sel[b, b // NPT, b % NPT * CH:(b % NPT + 1) * CH] = 1
    out["sel"] = sel
    S = np.zeros((OCT, OCT, OCT), f)
    S[0, 0, 0] = 1
    for n in range(1, OCT):
        S[0, n, n] = S[n, 0, n] = 1
        S[n, n, 0] = -1
    for t in ((1, 2, 3), (1, 4, 5), (1, 7, 6), (2, 4, 6), (2, 5, 7), (3, 4, 7), (3, 6, 5)):
        for v in range(3):
            p_, q_, r_ = t[v], t[(v + 1) % 3], t[(v + 2) % 3]
            S[p_, q_, r_], S[q_, p_, r_] = 1, -1
    perm = np.zeros((OCT, OB, OCT, OCT, OB), f)
    for j in range(OCT):
        for n in range(OCT):
            for k in range(OCT):
                for d in range(OB):
                    perm[j, d, k, n, d] = S[j, n, k]
    out["perm"] = bf16_bits(perm.reshape(P, OCT, P))
    cf = np.zeros((P, CF_W), f)
    cf[:, C_ID:C_ID + P] = np.eye(P)
    cf[:, C_IO:C_IO + E] = np.arange(E)
    cf[:, C_MK:C_MK + NPT] = np.arange(P)[:, None] // CH == np.arange(NPT)
    cf[0:E, C_TRI:C_TRI + E] = np.triu(np.ones((E, E)))
    cf[:, C_THR:C_THR + 8] = np.append(np.arange(1, CHUNKS) * P, 2 * TOK)
    cf[:, C_ONE:C_ONE + P] = 1
    out["cf"] = cf
    cb = np.ones((P, CB_W), f)
    cb[:, B_UP:B_UP + P] = np.triu(np.ones((P, P)), 1)
    out["cb"] = bf16_bits(cb)
    rec = np.zeros((P, NT, 2, 4), np.int32)
    tok = np.arange(TOK).reshape(NT, P).T
    rec[:, :, :, 0] = tok[:, :, None]
    rec[:, :, :, 1] = tok[:, :, None]
    out["rec"] = rec
    pads = np.zeros((P, E, 4), np.int32)
    pads[:, :, 0] = PADROW
    pads[:, :, 1] = TOK + np.arange(P)[:, None]
    out["pads"] = pads.reshape(P, E * 4)
    return {k: np.ascontiguousarray(v) for k, v in out.items()}


def kernel(**inputs):
    import numpy as np
    import concourse.bacc as bacc
    from concourse.bass_utils import run_bass_kernel_spmd

    arrays = layouts({k: np.asarray(v) for k, v in inputs.items()})
    nc = bacc.Bacc("TRN2", target_bir_lowering=False, num_devices=1)
    a = {k: nc.dram_tensor(f"in_{k}", v.shape, mybir.dt.from_np(v.dtype), kind="ExternalInput").ap() for k, v in arrays.items()}
    a["out"] = nc.dram_tensor("out", (TOK + P, D), F32, kind="ExternalOutput").ap()
    build_adaln_ffn(nc, a)
    r = run_bass_kernel_spmd(nc, [{f"in_{k}": v for k, v in arrays.items()}], core_ids=[0])
    return r.results[0]["out"][0:TOK].reshape(NB, CH, D)
```

```python
import concourse.bass as bass
from concourse import mybir
from contextlib import ExitStack

F32 = mybir.dt.float32
F32R = mybir.dt.float32r
BF16 = mybir.dt.bfloat16
I32 = mybir.dt.int32
U32 = mybir.dt.uint32
ALU = mybir.AluOpType
ACT = mybir.ActivationFunctionType
AX = mybir.AxisListType

P = 128
NB, CH, D = 32, 32, 512
TOK = NB * CH
NT = TOK // P
NPT = P // CH
R = D // P
TAPS = 9
QW = P + 2
OCT = 8
IN8, HID8, OUT8 = D // OCT, 170, D // OCT
OB = P // OCT
HC = -(-HID8 // OB)
HALF = TOK // 2
TPH = NT // 2
BW = HC * IN8
KC = 8
E = 32
DC = D // P
U = 8
NW = 2 * U
EARLY, MIDDLE = 3, 12
LAG = 5
XU = 2
G0 = E // U
PACE = 12
CHUNKS = TOK // P
XMAX = 16
assert PACE >= U and G0 % 2 == 0 and 2 * TOK // P <= XMAX
PADROW = 1 << 20

C_ID = 0
C_IO = C_ID + P
C_MK = C_IO + E
C_TRI = C_MK + NPT
C_THR = C_TRI + E
C_ONE = C_THR + CHUNKS
CF_W = C_ONE + P
B_UP, B_ONE = 0, P
CB_W = 2 * P


GROUPS = {
    "nets": (("cond", NB), ("cwt", CH), ("w0", P), ("w1", P), ("w2", KC), ("b01", 2), ("rows", CH + KC)),
    "mix": (("perm", OCT * P // 2), ("wrep", CH * KC), ("bkr", KC)),
    "kept": (("cbf", CB_W // 2), ("gwt", DC * E), ("rec", NT * 2 * 4)),
}
NETS, MIX, KEPT = (sum(w for _, w in GROUPS[g]) for g in ("nets", "mix", "kept"))


def split(ap, group):
    out, at = [], 0
    for _, w in GROUPS[group]:
        out.append(ap[:, at:at + w])
        at += w
    return out


def build_adaln_ffn(nc, a):
    ctx = ExitStack()
    with ctx:
        def dram(name, shape, dt):
            return nc.dram_tensor(name, shape, dt, kind="Internal").ap()

        y_tab = dram("y_tab", (TOK, D), F32)
        slots = dram("slots", ((CHUNKS + 1) * P * E, 4), I32)
        slots_v = slots.rearrange("(c p e) w -> c p e w", p=P, e=E)

        cur = [-(-nc.sbuf_base // 32) * 32]

        def region(size):
            at = cur[0]
            cur[0] += -(-size // 32) * 32
            assert cur[0] <= nc.sbuf_usable_end, (cur[0], nc.sbuf_usable_end)
            return at

        def put(name, shape, dt, at):
            return nc.alloc_sbuf_tensor_at(name, shape, dt, offset=at)

        def own(name, shape, dt):
            n = 4 if dt != BF16 else 2
            for s in shape[1:]:
                n *= s
            return put(name, shape, dt, region(n))

        class Cursor:

            def __init__(self, at, size):
                self.at, self.end = at, at + size

            def put(self, name, shape, dt):
                n = 4 if dt != BF16 else 2
                for s in shape[1:]:
                    n *= s
                t = put(name, shape, dt, self.at)
                self.at += -(-n // 32) * 32
                assert self.at <= self.end, name
                return t

        MB = R * HC * P * 4
        YB = R * TOK * 4
        r_w = region(EARLY * DC * D * 4)
        r_m = region(2 * MB)
        mg = put("mg", [P, R, HC, P], F32R, r_m)
        mu = put("mu", [P, R, HC, P], F32R, r_m + MB)
        r_y = region(2 * YB)
        y0hi = put("y0hi", [P, R, TOK], F32R, r_y)
        y0lo = put("y0lo", [P, R, TOK], F32R, r_y + YB)
        r_h = region(2 * HC * HALF * 4)
        hhi = put("hhi", [P, HC, HALF], F32R, r_h)
        hlo = put("hlo", [P, HC, HALF], F32R, r_h + HC * HALF * 4)
        md = own("md", [P, HC, D], F32R)
        acc = own("acc", [P, NT, D], F32)
        r_t = region(4 * D * 4)
        stmp = put("stmp", [P, 2, D], F32, r_t)
        htmp = put("htmp", [P, 2, D], F32, r_t + 2 * D * 4)
        combT = put("combT", [E, NT, P], F32, r_t)
        r_yr = region(2 * D * 4)
        yv = put("yv", [P, 2, D], F32, r_yr)
        yT = own("yT", [P, DC, P], F32)
        su = Cursor(r_h, 2 * HC * HALF * 4)
        xp = su.put("xp", [P, NB, QW], F32)
        base = su.put("base", [P, 3, BW], F32)
        wc = su.put("wc", [P, 3, P], F32)
        nets = su.put("nets", [P, NETS], F32)
        cb = su.put("cb", [P, NB, CH], F32)
        diag = su.put("diag", [NB, NB, CH], F32)
        sel = su.put("sel", [NB, NT, P], F32)
        cond, cwt, w0s, w1s, w2s, b01, rows = split(nets[:], "nets")
        h1, h2 = (su.put(n, [P, NB], F32) for n in ("h1", "h2"))
        asum = su.put("asum", [P, 3], F32)
        low = put("low", [P, BW], F32, r_t)
        mag = put("mag", [P, BW], F32, r_t + 2 * D * 4)
        sw = Cursor(r_w, EARLY * DC * D * 4)
        tern = sw.put("tern", [P, 3, BW], BF16)
        mix = sw.put("mix", [P, MIX], F32)
        perm, wrep, bkr = split(mix[:], "mix")
        perm = perm.bitcast(BF16).rearrange("p (k o) -> p k o", k=OCT)
        wrep = wrep.rearrange("p (o k) -> p o k", k=KC)
        prod = sw.put("prod", [P, CH, KC], F32)
        aggt = sw.put("aggt", [P, CH], F32)
        convt = put("convt", [P, 2, R, P], F32, r_yr)
        ex = Cursor(r_w, EARLY * DC * D * 4 + 2 * MB + 2 * YB + 2 * HC * HALF * 4 + HC * D * 4)
        wbuf = ex.put("wbuf", [P, NW, DC, D], F32)
        yg = [ex.put(f"yg{i}", [P, D], F32) for i in range(U)]
        xT = [ex.put(f"xT{i}", [P, DC, P], F32) for i in range(2)]
        res = [ex.put(f"res{i}", [P, D], F32) for i in range(U)]
        recs = ex.put("recs", [P, E + XU, 4], I32)
        cf = own("cf", [P, CF_W], F32)
        kept = own("kept", [P, KEPT], F32)
        cbf, gwt, rec = split(kept[:], "kept")
        cbf = cbf.bitcast(BF16)
        gwt = gwt.rearrange("p (c e) -> p c e", e=E)
        rec = rec.bitcast(I32).rearrange("p (j k w) -> p j k w", k=2, w=4)
        eb = own("eb", [E, D], F32)
        bd = own("bd", [P, NT, P], F32)
        src = own("src", [P, U], I32)
        dst = own("dst", [P, U, 2], I32)
        amat = own("amat", [P, NT, E], BF16)
        att = own("att", [NB, KC], F32)
        sm = own("sm", [NB, 4], F32)
        attx = own("attx", [P, NT, KC], F32)
        aggb = own("aggb", [P, NT], F32)
        wsc = own("wsc", [P, 3], F32)
        thr = own("thr", [P, 3], F32)
        nthr = own("nthr", [P, 3], F32)
        sud = own("sud", [P, 1], F32)
        lg = own("lg", [P, E], F32)
        mx = own("mx", [P, 8], F32)
        ix = own("ix", [P, 8], U32)
        oh = own("oh", [P, 2, E], F32)
        gap_th = own("gap_th", [P, 2], F32)
        gap, th = gap_th[:, 0:1], gap_th[:, 1:2]
        comb = own("comb", [P, NT, E], F32)
        junk = own("junk", [P, E], F32)
        sidf = own("sidf", [P, 2], F32)
        sid = own("sid", [P, NT, 2], I32)
        counts = own("counts", [E, 2], F32)
        cnt, incl = counts[:, 0:1], counts[:, 1:2]
        more = own("more", [E, 1], F32)
        before = own("before", [E, XMAX], F32)
        lst = own("lst", [1, 2 * XMAX + 1 + XMAX], F32)
        todo = own("todo", [1, 2 * XMAX + 1], I32)

        bank = [ctx.enter_context(nc.psum_tensor(f"bank{i}", [P, 512], F32)) for i in range(8)]
        CONV = bank[0:2]
        CBB = bank[2:4]
        PG, PU = bank[2:4], bank[5:7]
        PD = (bank[4], bank[7])
        G, UU, DN = bank[0:2], bank[2:4], bank[5:7]
        BY, BT = bank[4], bank[7]
        EBB = (DN[0], G[1], UU[1], DN[1])
        XT, RS = bank[0:2], bank[2:4]

        def logit_bank(j):
            return DN[0] if j == TPH - 1 else G[0]

        def position_bank(j):
            return DN[0] if j in (TPH - 2, TPH - 1) else UU[0]

        def sem(name):
            return ctx.enter_context(nc.semaphore(name))

        wc_in, cf_in, nets_in, mix_in, sel_in, kept_in, eb_in = (
            sem(s) for s in ("wc_in", "cf_in", "nets_in", "mix_in", "sel_in", "kept_in", "eb_in"))
        base_in = [sem(f"base_in{m}") for m in range(3)]
        XPG = (0, 1, 2, 4, 8)
        xp_in = [sem(f"xp_in{g}") for g in range(len(XPG) - 1)]
        acc_in = sem("acc_in")
        pads_in = sem("pads_in")
        w_in = [sem(f"w_in{u}") for u in range(U)]
        dve_chain = sem("dve_chain")
        ctx_mm, diag_done, cb_mm, cb_done = (sem(s) for s in ("ctx_mm", "diag_done", "cb_mm", "cb_done"))
        h1_mm, h1_done, h2_mm, h2_done = (sem(s) for s in ("h1_mm", "h1_done", "h2_mm", "h2_done"))
        att_mm, att_max, att_exp, att_done = (sem(s) for s in ("att_mm", "att_max", "att_exp", "att_done"))
        attx_mm, attx_done, mix_done = (sem(s) for s in ("attx_mm", "attx_done", "mix_done"))
        asum_done, scale_mm, thr_done, tern_done = (sem(s) for s in ("asum_done", "scale_mm", "thr_done", "tern_done"))
        pg_mm, pg_done, pu_mm, pu_done, pd_mm, pd_done = (sem(s) for s in ("pg_mm", "pg_done", "pu_mm", "pu_done", "pd_mm", "pd_done"))
        conv_mm, convt_done, y0hi_done, y0lo_done = (sem(s) for s in ("conv_mm", "convt_done", "y0hi_done", "y0lo_done"))
        g_mm, u_mm, silu_done, h_done, hhi_done, hlo_done = (sem(s) for s in ("g_mm", "u_mm", "silu_done", "h_done", "hhi_done", "hlo_done"))
        d_mm, acc_done = sem("d_mm"), sem("acc_done")
        y_mm, y_done, yt_mm, yt_done, lg_mm = (sem(s) for s in ("y_mm", "y_done", "yt_mm", "yt_done", "lg_mm"))
        y_stored = [sem(f"y_stored{i}") for i in range(2)]
        gap_done, th_done, choice_done, pos_mm, slots_done, combt_done, eb_mm, acc2_done = (
            sem(s) for s in ("gap_done", "th_done", "choice_done", "pos_mm", "slots_done", "combt_done", "eb_mm", "acc2_done"))
        recs_out = sem("recs_out")
        combt_mm, amat_done = sem("combt_mm"), sem("amat_done")
        cnt_mm, more_done, incl_mm, before_done, list_mm, todo_done = (
            sem(s) for s in ("cnt_mm", "more_done", "incl_mm", "before_done", "list_mm", "todo_done"))
        recs_in, src_ready, dst_ready = sem("recs_in"), sem("src_ready"), sem("dst_ready")
        further_in = [sem(f"further_in{u}") for u in range(XU)]
        yg_in = [sem(f"yg_in{b}") for b in range(U)]
        res_out = sem("res_out")
        yg_zero, pool_steps, sp_steps = sem("yg_zero"), sem("pool_steps"), sem("sp_steps")
        xt_mm, xt_done, r_mm, res_done = (sem(s) for s in ("xt_mm", "xt_done", "r_mm", "res_done"))
        out_base = sem("out_base")

        ident = cf[:, C_ID:C_ID + P]
        iota = cf[:, C_IO:C_IO + E]
        bmask = cf[:, C_MK:C_MK + NPT]
        ones = cf[:, C_ONE:C_ONE + P]

        block = ctx.enter_context(nc.Block())

        TABLES = 2 * OCT
        BATCHES = [(g, b) for g in range(2, NT) for b in range(NPT)]

        def batches_by(i):
            return min(len(BATCHES), (i + 1) * len(BATCHES) // (TABLES - 1))

        CONV_BESIDE = {i // 2: 1 + batches_by(i) // NPT for i in range(TABLES)
                       if batches_by(i) // NPT > batches_by(i - 1) // NPT}

        @block.sync
        def _(sp):
            sp.dma_start(wc[:], a["wc"]).then_inc(wc_in, 16)
            for n, (g0, g1) in enumerate(zip(XPG, XPG[1:])):
                sp.dma_start(xp[:, NPT * g0:NPT * g1], a["xp"][:, NPT * g0:NPT * g1]).then_inc(xp_in[n], 16)
                if n == 0:
                    for m in range(3):
                        sp.dma_start(base[:, m], a["base"][:, m]).then_inc(base_in[m], 16)
                    sp.dma_start(mix[:], a["mix"]).then_inc(mix_in, 16)
            sp.dma_start(sel[:], a["sel"]).then_inc(sel_in, 16)
            sp.dma_start(kept[:], a["kept"]).then_inc(kept_in, 16)
            sp.dma_start(eb[:], a["eb"]).then_inc(eb_in, 16)
            sp.dma_start(acc[:], a["x"].rearrange("(j p) d -> p j d", p=P)).then_inc(acc_in, 16)
            sp.dma_start(slots.rearrange("(c p e) w -> p c (e w)", p=P, e=E),
                         a["pads"].unsqueeze(1).to_broadcast([P, CHUNKS + 1, 4 * E])).then_inc(pads_in, 16)

            def load_w(e, b, u):
                for c in range(DC):
                    sp.dma_start(wbuf[:, bass.ds(b, 1), c], a["w"][bass.ds(e, 1), :, c].rearrange("a p d -> p a d")).then_inc(w_in[u], 16)

            sp.wait_ge(pd_mm, OCT)
            sp.wait_ge(mix_done, NT)
            for t in range(EARLY):
                load_w(t, t, t % U)

            def store_y(j):
                sp.wait_ge(y_done, j + 1)
                sp.dma_start(y_tab[P * j:P * (j + 1)], yv[:, j % 2]).then_inc(y_stored[j % 2], 16)

            for j in range(NT):
                if j == TPH:
                    sp.wait_ge(u_mm, 2 * HC)
                    sp.wait_ge(g_mm, 2 * HC)
                if TPH <= j < NT - 1:
                    for t in range(EARLY, MIDDLE):
                        if (t - EARLY) * (TPH - 1) // (MIDDLE - EARLY) == j - TPH:
                            if t >= U:
                                sp.wait_ge(w_in[t % U], 64)
                            load_w(t, t, t % U)
                store_y(j)

            sp.wait_ge(recs_out, 2 * NT * 16)
            sp.dma_start(recs[:, 0:E], slots_v[0]).then_inc(recs_in, 16)
            sp.wait_ge(yg_in[0], 16)
            for j in range(NT):
                sp.wait_ge(acc2_done, j + 1)
                sp.dma_start(a["out"][P * j:P * (j + 1)], acc[:, j]).then_inc(out_base, 16)
            sp.dma_start(a["out"][TOK:TOK + P], acc[:, 0]).then_inc(out_base, 16)
            for t in range(MIDDLE, NW):
                sp.wait_ge(r_mm, t - MIDDLE + 1)
                sp.wait_ge(w_in[t % U], 64)
                load_w(t, t, t % U)

            def load_further(e, c, u):
                sp.dma_start(recs[:, E + u], slots_v[bass.ds(c, 1), :, bass.ds(e, 1), :].rearrange("c p e w -> (c p) (e w)")).then_inc(further_in[u], 16)

            sp.wait_ge(todo_done, 1)
            bodies = sp.value_load(todo[0:1, 2 * XMAX:2 * XMAX + 1], min_val=0, max_val=XMAX // XU - 1)
            further = []
            for u in range(XU):
                e = sp.value_load(todo[0:1, u:u + 1], min_val=0, max_val=E - 1)
                c = sp.value_load(todo[0:1, XMAX + u:XMAX + u + 1], min_val=0, max_val=CHUNKS)
                load_further(e, c, u)
                further.append(e)
            with sp.Fori(1, G0 - 1) as g:
                for u in range(U):
                    sp.wait_ge(r_mm, g * PACE + (u * PACE // U - PACE // 2))
                    sp.wait_ge(w_in[u], g * 64 + 64)
                    load_w(g * U + (U + u), (g + 1) % 2 * U + u, u)
            for u in range(XU):
                sp.wait_ge(r_mm, (G0 - 1) * PACE + u * PACE // U - PACE // 2)
                sp.wait_ge(w_in[u], 64 * G0)
                load_w(further[u], u, u)
            with sp.If(bodies > 0):
                with sp.Fori(1, bodies + 1) as g:
                    for u in range(XU):
                        e = sp.value_load(todo[0:1, bass.ds(g * XU + u, 1)], min_val=0, max_val=E - 1)
                        c = sp.value_load(todo[0:1, bass.ds(g * XU + (u + XMAX), 1)], min_val=0, max_val=CHUNKS)
                        sp.wait_ge(dst_ready, g * XU + (E + u - XU + 1))
                        load_further(e, c, u)
                        sp.wait_ge(r_mm, g * XU + (E + u - XU + 1))
                        load_w(e, u, u)
            sp.wait_ge(res_out, bodies * (16 * XU) + 16 * (E + XU))
            sp.sem_inc(sp_steps, 1)
            sp.wait_ge(out_base, 16 * (NT + 1))

        @block.gpsimd
        def _(pool):
            for g in range(NT):
                pool.wait_ge(y0hi_done, g + 1)
                nc.gpsimd.tensor_tensor(y0lo[:, :, P * g:P * (g + 1)], convt[:, g % 2], y0hi[:, :, P * g:P * (g + 1)].bitcast(F32), ALU.subtract).then_inc(y0lo_done, 1)
            pool.wait_ge(pads_in, 16)
            pool.wait_ge(kept_in, 16)
            for j in range(NT):
                if j == NT - 2:
                    pool.wait_ge(d_mm, NT)
                    for b in range(U):
                        nc.gpsimd.memset(yg[b][:], 0.0).then_inc(yg_zero, 1)
                    pool.wait_ge(yg_zero, U)
                pool.wait_ge(slots_done, j + 1)
                for k in range(2):
                    pool.indirect_dma_start(out=slots, out_offset=bass.IndirectOffsetOnAxis(ap=sid[:, j, k:k + 1], axis=0),
                                            in_=rec[:, j, k], in_offset=None).then_inc(recs_out, 16)
            for i in range(2):
                pool.wait_ge(y_stored[i], NT // 2 * 16)

            last_token, last_row = pool.to_reg(TOK - 1), pool.to_reg(TOK + P - 1)

            def gather(t, b):
                pool.wait_ge(src_ready, t + 1)
                pool.sem_inc(pool_steps, 1)
                pool.indirect_dma_start(out=yg[b][:], out_offset=None, in_=y_tab,
                                        in_offset=bass.IndirectOffsetOnAxis(ap=src[:, b:b + 1].bitcast(U32), axis=0),
                                        bounds_check=last_token, oob_is_err=False).then_inc(yg_in[b], 16)

            def scatter(t, b):
                pool.wait_ge(res_done, t + 1)
                if not (isinstance(t, int) and t == 0):
                    pool.wait_ge(res_out, t * 16)
                pool.sem_inc(pool_steps, 1)
                pool.indirect_dma_start(out=a["out"], out_offset=bass.IndirectOffsetOnAxis(ap=dst[:, b, 0:1].bitcast(U32), axis=0),
                                        in_=res[b][:], in_offset=None, compute_op=ALU.add,
                                        bounds_check=last_row).then_inc(res_out, 16)

            for t in range(U):
                gather(t, t)
                if t == LAG:
                    pool.wait_ge(out_base, 16 * (NT + 1))
                if t >= LAG:
                    scatter(t - LAG, t - LAG)
            with pool.Fori(1, G0) as g:
                for u in range(U):
                    gather(g * U + u, u)
                    scatter(g * U + (u - LAG), (u - LAG) % U)
            for u in range(XU):
                gather(E + u, u)
                scatter(E + u - LAG, (u - LAG) % U)
            for t in range(E + XU - LAG, E + XU):
                scatter(t, t % U)
            pool.wait_ge(todo_done, 1)
            bodies = pool.value_load(todo[0:1, 2 * XMAX:2 * XMAX + 1], min_val=0, max_val=XMAX // XU - 1)
            with pool.If(bodies > 0):
                with pool.Fori(1, bodies + 1) as g:
                    for u in range(XU):
                        gather(g * XU + (E + u), u)
                    for u in range(XU):
                        scatter(g * XU + (E + u), u)

        @block.scalar
        def _(act):
            act.dma_start(nets[:], a["nets"]).then_inc(nets_in, 16)
            act.dma_start(cf[:], a["cf"]).then_inc(cf_in, 16)
            for m in range(3):
                act.wait_ge(base_in[m], 16)
                if m:
                    act.wait_ge(asum_done, m)
                nc.scalar.activation(mag[:], base[:, m], ACT.Abs, accum_out=asum[:, m:m + 1]).then_inc(asum_done, 1)
            for hm, bcol, h, hd in ((h1_mm, 0, h1, h1_done), (h2_mm, 1, h2, h2_done)):
                act.wait_ge(hm, 1)
                nc.scalar.activation(h[:], BY[:, NB * bcol:NB * (bcol + 1)], ACT.Gelu, bias=b01[:, bcol:bcol + 1]).then_inc(hd, 1)
                if bcol == 0:
                    act.wait_ge(cb_mm, 1)
                    for h_ in range(2):
                        nc.scalar.activation(cb[:].rearrange("p n c -> p (n c)")[:, 512 * h_:512 * (h_ + 1)], CBB[h_][:], ACT.Copy).then_inc(cb_done, 1)

            def conv_hi(g):
                act.wait_ge(convt_done, g + 1)
                nc.scalar.activation(y0hi[:, :, P * g:P * (g + 1)], convt[:, g % 2], ACT.Copy).then_inc(y0hi_done, 1)

            def gate_table(k):
                act.wait_ge(pg_mm, k + 1)
                for h_ in range(2):
                    v = nc.scalar.activation(mg[:, 2 * h_:2 * h_ + 2, :, OB * k:OB * (k + 1)],
                                             PG[h_][:, 0:BW // 2].rearrange("p (r c o) -> p r c o", r=2, o=OB), ACT.Copy)
                v.then_inc(pg_done, 1)

            def down_table(k):
                act.wait_ge(pd_mm, k + 1)
                for h_, (c0, c1) in enumerate(((0, 6), (6, HC))):
                    v = nc.scalar.activation(md[:, c0:c1, OUT8 * k:OUT8 * (k + 1)],
                                             PD[h_][:, 0:(c1 - c0) * OUT8].rearrange("p (c o) -> p c o", o=OUT8), ACT.Copy)
                v.then_inc(pd_done, 1)

            conv_hi(0)
            for g in range(NT):
                gate_table(g)
                if g == 0:
                    conv_hi(1)
                if g in CONV_BESIDE:
                    conv_hi(CONV_BESIDE[g])
                if g == 1:
                    act.wait_ge(att_max, 1)
                    nc.scalar.activation(att[:], BY[0:NB, 64:64 + KC], ACT.Exp, bias=sm[:, 1:2], accum_out=sm[:, 2:3]).then_inc(att_exp, 1)
                if g == 4:
                    act.wait_ge(attx_mm, 1)
                    nc.scalar.activation(attx[:].rearrange("p g k -> p (g k)"), BT[:, 64:64 + NT * KC], ACT.Copy).then_inc(attx_done, 1)

            def silu(n):
                act.wait_ge(g_mm, n + 1)
                if n >= 2:
                    act.wait_ge(h_done, n - 1)
                nc.scalar.activation(stmp[:, n % 2], G[n % 2][:], ACT.Silu, scale=wsc[:, 0:1]).then_inc(silu_done, 1)

            def hid_hi(n):
                act.wait_ge(h_done, n + 1)
                nc.scalar.activation(hhi[:, n % HC], htmp[:, n % 2], ACT.Copy).then_inc(hhi_done, 1)

            def y_evac(j):
                act.wait_ge(y_mm, j + 1)
                if j == 0:
                    act.wait_ge(y0lo_done, NT)
                if j >= 2:
                    act.wait_ge(y_stored[j % 2], j // 2 * 16)
                    act.wait_ge(yt_mm, j - 1)
                nc.scalar.activation(yv[:, j % 2], BY[:], ACT.Identity, bias=aggb[:, j:j + 1]).then_inc(y_done, 1)

            def yt_evac(j):
                act.wait_ge(yt_mm, j + 1)
                if j >= 1:
                    act.wait_ge(lg_mm, j)
                nc.scalar.activation(yT[:].rearrange("p c t -> p (c t)"), BT[:], ACT.Copy).then_inc(yt_done, 1)

            def combt_evac(half):
                act.wait_ge(combt_mm, half + 1)
                if half == 0:
                    act.wait_ge(hlo_done, 2 * HC)
                nc.scalar.activation(combT[:, TPH * half:TPH * (half + 1)].rearrange("e j t -> e (j t)"),
                                     (G[1], BY)[half][0:E, :], ACT.Copy).then_inc(combt_done, 1)

            def weight_tanh(j):
                act.wait_ge(gap_done, j + 1)
                nc.scalar.activation(th, gap, ACT.Tanh, scale=0.5).then_inc(th_done, 1)

            act.wait_ge(tern_done, 3)
            for half in range(2):
                for c in range(HC):
                    n = half * HC + c
                    if half == 0 and 1 <= c <= OCT:
                        down_table(c - 1)
                    silu(n)
                    if c >= 1:
                        hid_hi(n - 1)
                    if half == 1:
                        if c == 0:
                            y_evac(TPH - 1)
                        if c == 3:
                            yt_evac(TPH - 1)
                        if c == 6:
                            weight_tanh(TPH - 1)
                hid_hi(half * HC + HC - 1)
                for t in range(1, TPH):
                    j = half * TPH + t
                    y_evac(j - 1)
                    if t >= 2:
                        weight_tanh(j - 2)
                    yt_evac(j - 1)
                if half == 0:
                    weight_tanh(TPH - 2)
            combt_evac(0)
            weight_tanh(NT - 2)
            y_evac(NT - 1)
            yt_evac(NT - 1)
            weight_tanh(NT - 1)
            combt_evac(1)

            def evac(t, b):
                act.wait_ge(dst_ready, t + 1)
                act.wait_ge(r_mm, t + 1)
                nc.scalar.activation(res[b][:], RS[b % 2][:], ACT.Copy, scale=dst[:, b, 1:2].bitcast(F32)).then_inc(res_done, 1)

            for t in range(U):
                evac(t, t)
            with act.Fori(1, G0) as g:
                for u in range(U):
                    evac(g * U + u, u)
            for u in range(XU):
                evac(E + u, u)
            act.wait_ge(todo_done, 1)
            bodies = act.value_load(todo[0:1, 2 * XMAX:2 * XMAX + 1], min_val=0, max_val=XMAX // XU - 1)
            with act.If(bodies > 0):
                with act.Fori(1, bodies + 1) as g:
                    for u in range(XU):
                        evac(g * XU + (E + u), u)

        @block.vector
        def _(dve):
            chain = [0]

            def link(*results):
                for ins in results:
                    chain[0] += 1
                    ins.then_inc(dve_chain, 1)
                dve.wait_ge(dve_chain, chain[0])

            dve.wait_ge(cf_in, 16)
            dve.wait_ge(ctx_mm, 1)
            nc.vector.tensor_tensor(diag[:], BT[0:NB, 0:CH].unsqueeze(1).to_broadcast([NB, NB, CH]),
                                    ident[0:NB, 0:NB].unsqueeze(2).to_broadcast([NB, NB, CH]), ALU.mult).then_inc(diag_done, 1)

            def scales(m0, m1):
                dve.wait_ge(scale_mm, min(m0 + 1, 2))
                link(nc.vector.tensor_scalar(wsc[:, m0:m1], BT[:, 32 + m0:32 + m1], 1.0 / (OCT * HID8 * IN8), None, ALU.mult))
                nc.vector.engine_nop().then_inc(thr_done, 1)
                link(nc.vector.tensor_scalar(thr[:, m0:m1], wsc[:, m0:m1], 0.5, None, ALU.mult),
                     nc.vector.tensor_scalar(nthr[:, m0:m1], wsc[:, m0:m1], -0.5, None, ALU.mult))

            def quantize(m):
                link(nc.vector.tensor_scalar(low[:], base[:, m], nthr[:, m:m + 1], None, ALU.is_lt))
                nc.vector.scalar_tensor_tensor(tern[:, m], base[:, m], thr[:, m:m + 1], low[:], ALU.is_gt, ALU.subtract).then_inc(tern_done, 1)
                dve.wait_ge(tern_done, m + 1)

            def conv_evac(g):
                dve.wait_ge(conv_mm, g + 1)
                if g == 0:
                    dve.wait_ge(cb_done, 2)
                if g >= 2:
                    dve.wait_ge(y0hi_done, g - 1)
                    dve.wait_ge(y0lo_done, g - 1)
                nc.vector.tensor_tensor(convt[:, g % 2].rearrange("p r (n c) -> p r n c", c=CH),
                                        CONV[g % 2][:].rearrange("p (n r c) -> p r n c", n=NPT, c=CH),
                                        cb[:, NPT * g:NPT * (g + 1)].unsqueeze(1).to_broadcast([P, R, NPT, CH]), ALU.add).then_inc(convt_done, 1)

            def up_table(k):
                dve.wait_ge(pu_mm, k + 1)
                for h_ in range(2):
                    v = nc.vector.tensor_copy(mu[:, 2 * h_:2 * h_ + 2, :, OB * k:OB * (k + 1)],
                                              PU[h_][:, 0:BW // 2].rearrange("p (r c o) -> p r c o", r=2, o=OB))
                v.then_inc(pu_done, 1)

            def mixed_kernel(t):
                link(nc.vector.tensor_tensor(prod[:], wrep, attx[:, t].unsqueeze(1).to_broadcast([P, CH, KC]), ALU.mult))
                link(nc.vector.tensor_reduce(aggt[:], prod[:], AX.X, ALU.add))
                nc.vector.tensor_tensor(bd[:, t].rearrange("p (b o) -> p b o", b=NPT),
                                        aggt[:].unsqueeze(1).to_broadcast([P, NPT, CH]),
                                        bmask.unsqueeze(2).to_broadcast([P, NPT, CH]), ALU.mult).then_inc(mix_done, 1)
                dve.wait_ge(mix_done, t + 1)

            scales(0, 1)
            quantize(0)
            conv_evac(0)
            scales(1, 3)
            nc.vector.tensor_tensor(sud[:], wsc[:, 1:2], wsc[:, 2:3], ALU.mult).then_inc(dve_chain, 1)
            chain[0] += 1
            quantize(1)
            conv_evac(1)
            for g in range(NT):
                up_table(g)
                if g in CONV_BESIDE:
                    conv_evac(CONV_BESIDE[g])
                if g == 0:
                    quantize(2)
                if g == 1:
                    dve.wait_ge(att_mm, 1)
                    link(nc.vector.reduce_max(sm[:, 0:1], BY[0:NB, 64:64 + KC], axis=AX.X))
                    nc.vector.tensor_scalar(sm[:, 1:2], sm[:, 0:1], -1.0, None, ALU.mult).then_inc(att_max, 1)
                if g == 2:
                    dve.wait_ge(att_exp, 1)
                    link(nc.vector.reciprocal(sm[:, 3:4], sm[:, 2:3]))
                    nc.vector.tensor_scalar(att[:], att[:], sm[:, 3:4], None, ALU.mult).then_inc(att_done, 1)
                if g == NT - 1:
                    dve.wait_ge(attx_done, 1)
                    dve.wait_ge(mix_in, 16)
                    link(nc.vector.tensor_tensor(prod[:, 0:NT, :], attx[:], bkr.unsqueeze(1).to_broadcast([P, NT, KC]), ALU.mult))
                    link(nc.vector.tensor_reduce(aggb[:], prod[:, 0:NT, :], AX.X, ALU.add))

            def hidden(n):
                dve.wait_ge(silu_done, n + 1)
                dve.wait_ge(u_mm, n + 1)
                if n >= 2:
                    dve.wait_ge(hhi_done, n - 1)
                    dve.wait_ge(hlo_done, n - 1)
                nc.vector.tensor_tensor(htmp[:, n % 2], UU[n % 2][:], stmp[:, n % 2], ALU.mult).then_inc(h_done, 1)

            def hid_lo(n):
                dve.wait_ge(hhi_done, n + 1)
                nc.vector.tensor_tensor(hlo[:, n % HC], htmp[:, n % 2], hhi[:, n % HC].bitcast(F32), ALU.subtract).then_inc(hlo_done, 1)

            def acc_evac(j):
                if j == 0:
                    dve.wait_ge(acc_in, 16)
                dve.wait_ge(d_mm, j + 1)
                nc.vector.scalar_tensor_tensor(acc[:, j], DN[j % 2][:], sud[:, 0:1], acc[:, j], ALU.mult, ALU.add).then_inc(acc_done, 1)

            def choose(j):
                dve.wait_ge(lg_mm, j + 1)
                link(nc.vector.max(mx[:], logit_bank(j)[:, 0:E]))
                nc.vector.tensor_tensor(gap, mx[:, 0:1], mx[:, 1:2], ALU.subtract).then_inc(gap_done, 1)
                link(nc.vector.max_index(ix[:], mx[:], logit_bank(j)[:, 0:E]))
                link(nc.vector.tensor_scalar(oh[:, 0], iota, ix[:, 0:1], None, ALU.is_equal),
                     nc.vector.tensor_scalar(oh[:, 1], iota, ix[:, 1:2], None, ALU.is_equal))
                nc.vector.tensor_tensor(amat[:, j], oh[:, 0], oh[:, 1], ALU.add).then_inc(amat_done, 1)

            def weigh(j):
                dve.wait_ge(th_done, j + 1)
                link(*(nc.vector.tensor_scalar(rec[:, j, k, 2:3].bitcast(F32), th, s, 0.5, ALU.mult, ALU.add) for k, s in ((0, 0.5), (1, -0.5))))
                link(nc.vector.tensor_scalar(comb[:, j], oh[:, 0], rec[:, j, 0, 2:3].bitcast(F32), None, ALU.mult))
                nc.vector.scalar_tensor_tensor(comb[:, j], oh[:, 1], rec[:, j, 1, 2:3].bitcast(F32), comb[:, j], ALU.mult, ALU.add).then_inc(choice_done, 1)

            def place(j):
                dve.wait_ge(pos_mm, j + 1)
                link(nc.vector.scalar_tensor_tensor(lg[:], position_bank(j)[:, E:2 * E], float(E), iota, ALU.mult, ALU.add))
                for k in range(2):
                    link(nc.vector.scalar_tensor_tensor(junk[:], iota, ix[:, k:k + 1], lg[:], ALU.is_equal, ALU.mult, accum_out=sidf[:, k:k + 1]))
                nc.vector.tensor_copy(sid[:, j], sidf[:]).then_inc(slots_done, 1)
                dve.wait_ge(slots_done, j + 1)

            def add_bias(j):
                dve.wait_ge(eb_mm, j + 1)
                nc.vector.tensor_tensor(acc[:, j], acc[:, j], EBB[j % TPH][:], ALU.add).then_inc(acc2_done, 1)

            dve.wait_ge(kept_in, 16)
            for half in range(2):
                for c in range(HC):
                    n = half * HC + c
                    hidden(n)
                    if c >= 1:
                        hid_lo(n - 1)
                    if half == 0 and 1 <= c <= NT:
                        mixed_kernel(c - 1)
                    if half == 1:
                        if c == 2:
                            place(TPH - 2)
                        if c == 5:
                            choose(TPH - 1)
                        if c == 6:
                            weigh(TPH - 1)
                        if c == 8:
                            place(TPH - 1)
                hid_lo(half * HC + HC - 1)
                for t in range(TPH):
                    j = half * TPH + t
                    if t >= 2:
                        choose(j - 2)
                        weigh(j - 2)
                        place(j - 2)
                    if j == NT - 1:
                        choose(j - 1)
                    acc_evac(j)
                if half == 0:
                    choose(TPH - 2)
                    weigh(TPH - 2)
            weigh(NT - 2)
            place(NT - 2)
            choose(NT - 1)
            weigh(NT - 1)
            place(NT - 1)
            for j in range(TPH):
                add_bias(j)
            dve.wait_ge(recs_in, 16)
            nc.vector.tensor_copy(src[:], recs[:, 0:U, 0]).then_inc(src_ready, U)
            nc.vector.tensor_copy(dst[:], recs[:, 0:U, 1:3]).then_inc(dst_ready, U)
            for j in range(TPH, NT):
                add_bias(j)

            def xt_evac(i, u, first=False):
                dve.wait_ge(xt_mm, i + 1)
                if not first:
                    dve.wait_ge(r_mm, i - 1)
                nc.vector.tensor_copy(xT[u % 2][:].rearrange("p c t -> p (c t)"), XT[u % 2][:]).then_inc(xt_done, 1)

            def take_src(r, u):
                nc.vector.tensor_copy(src[:, u:u + 1], recs[:, bass.ds(r, 1), 0]).then_inc(src_ready, 1)

            def take_dst(r, u, scattered=None):
                if scattered is not None:
                    dve.wait_ge(res_out, scattered)
                nc.vector.tensor_copy(dst[:, u], recs[:, bass.ds(r, 1), 1:3].rearrange("p a w -> p (a w)")).then_inc(dst_ready, 1)

            xt_evac(0, 0, True)
            take_src(U, 0)
            xt_evac(1, 1, True)
            take_src(U + 1, 1)
            dve.wait_ge(cnt_mm, 1)
            link(nc.vector.tensor_copy(cnt, BY[0:E, 0:1]))
            nc.vector.tensor_scalar(junk[0:E, 0:8], cf[0:E, C_THR:C_THR + 8], cnt, 0.0, ALU.is_lt, ALU.add, accum_out=more[:]).then_inc(more_done, 1)
            dve.wait_ge(incl_mm, 1)
            link(nc.vector.tensor_copy(incl, BY[0:E, 0:1]))
            nc.vector.tensor_scalar(before[:], iota[0:E, 0:XMAX], incl, None, ALU.is_ge).then_inc(before_done, 1)
            dve.wait_ge(list_mm, 1)
            ends = lst[:, 2 * XMAX + 1:]
            link(nc.vector.tensor_copy(lst[:, 0:2 * XMAX + 1], BY[0:1, 0:2 * XMAX + 1]))
            link(nc.vector.tensor_scalar(ends, lst[:, 0:XMAX], float(E), None, ALU.is_ge))
            link(nc.vector.tensor_tensor(lst[:, 0:XMAX], lst[:, 0:XMAX], ends, ALU.subtract))
            link(nc.vector.scalar_tensor_tensor(lst[:, XMAX:2 * XMAX], iota[0:1, 0:XMAX], 1.0, lst[:, XMAX:2 * XMAX], ALU.add, ALU.subtract))
            link(nc.vector.scalar_tensor_tensor(junk[0:1, 0:XMAX], ends, float(CHUNKS), lst[:, XMAX:2 * XMAX], ALU.mult, ALU.max))
            link(nc.vector.tensor_copy(lst[:, XMAX:2 * XMAX], junk[0:1, 0:XMAX]))
            link(nc.vector.tensor_scalar(junk[0:1, 0:XMAX // XU - 1], cf[0:1, C_IO + XU:C_IO + XMAX:XU], lst[:, 2 * XMAX:2 * XMAX + 1], 0.0, ALU.is_lt, ALU.add,
                                         accum_out=lg[0:1, 0:1]))
            nc.vector.tensor_copy(todo[:, 2 * XMAX:2 * XMAX + 1], lg[0:1, 0:1]).then_inc(dve_chain, 1)
            chain[0] += 1
            link(nc.vector.tensor_copy(todo[:, 0:2 * XMAX], lst[:, 0:2 * XMAX]))
            nc.vector.engine_nop().then_inc(todo_done, 1)
            for t in range(2, U):
                xt_evac(t, t)
                take_src(U + t, t)
            with dve.Fori(1, G0 - 1) as g:
                for u in range(U):
                    xt_evac(g * U + u, u)
                    take_src(g * U + (U + u), u)
                    take_dst(g * U + u, u, g * (16 * U) + 16 * (u - U + 1))
            for t in range(E - U, E + XU):
                u = t % U
                xt_evac(t, u)
                if t + U < E + XU:
                    dve.wait_ge(further_in[u], 16)
                    take_src(t + U, u)
                take_dst(t, u, 16 * (t - U + 1))
            bodies = dve.value_load(todo[0:1, 2 * XMAX:2 * XMAX + 1], min_val=0, max_val=XMAX // XU - 1)
            with dve.If(bodies > 0):
                with dve.Fori(1, bodies + 1) as g:
                    for u in range(XU):
                        dve.wait_ge(further_in[u], g * 16 + 16)
                        take_src(E + u, u)
                    for u in range(XU):
                        xt_evac(g * XU + (E + u), u)
                        take_dst(E + u, u, g * (16 * XU) + 16 * (E + u - XU + 1))

        @block.tensor
        def _(pe):
            mm = nc.tensor.matmul

            def conv(g, b):
                if b == 0 and g in XPG:
                    pe.wait_ge(xp_in[XPG.index(g)], 16)
                if b == 0 and g >= 2:
                    pe.wait_ge(convt_done, g - 1)
                for s in range(3):
                    v = mm(CONV[g % 2][:, P * b:P * (b + 1)], xp[:, NPT * g + b, s:s + P], wc[:, s], start=(s == 0), stop=(s == 2))
                if b == NPT - 1:
                    v.then_inc(conv_mm, 1)

            def table(k, m, banks, made, used):
                if k >= 1:
                    pe.wait_ge(used, k)
                cut = BW // 2 if m < 2 else 6 * OUT8
                for h_, (c0, c1) in enumerate(((0, cut), (cut, BW))):
                    v = mm(banks[h_][:, 0:c1 - c0], perm[:, k], tern[:, m, c0:c1], start=True, stop=True)
                v.then_inc(made, 1)

            pe.wait_ge(wc_in, 16)
            conv(0, 0)
            pe.wait_ge(nets_in, 16)
            pe.wait_ge(cf_in, 16)
            mm(BT[0:NB, 0:CH], cond, cwt, start=True, stop=False)
            mm(BT[0:NB, 0:CH], ones[0:1, 0:NB], rows[0:1, 0:CH], start=False, stop=True).then_inc(ctx_mm, 1)
            mm(BY[:, 0:NB], w0s, cond, start=True, stop=True).then_inc(h1_mm, 1)
            for b in range(1, NPT):
                conv(0, b)

            def scale(m0, m1):
                pe.wait_ge(asum_done, m1)
                mm(BT[:, 32 + m0:32 + m1], ones, asum[:, m0:m1], start=True, stop=True).then_inc(scale_mm, 1)

            pe.wait_ge(diag_done, 1)
            scale(0, 1)
            for h_ in range(2):
                v = mm(CBB[h_][:], ones[0:NB, :], diag[:].rearrange("b n c -> b (n c)")[:, 512 * h_:512 * (h_ + 1)], start=True, stop=True)
            v.then_inc(cb_mm, 1)
            for b in range(2):
                conv(1, b)
            pe.wait_ge(thr_done, 1)
            scale(1, 3)
            pe.wait_ge(h1_done, 1)
            mm(BY[:, NB:2 * NB], w1s, h1[:], start=True, stop=True).then_inc(h2_mm, 1)
            pe.wait_ge(cb_done, 2)
            pe.wait_ge(mix_in, 16)
            for g in range(OCT):
                for m, banks, made, used in ((0, PG, pg_mm, pg_done), (1, PU, pu_mm, pu_done)):
                    if g == 0:
                        pe.wait_ge(tern_done, m + 1)
                    table(g, m, banks, made, used)
                    if g == 0 and m == 0:
                        for b in range(2, NPT):
                            conv(1, b)
                    for tile, b in BATCHES[batches_by(2 * g + m - 1):batches_by(2 * g + m)]:
                        conv(tile, b)
                if g == 0:
                    pe.wait_ge(h2_done, 1)
                    mm(BY[0:NB, 64:64 + KC], h2[:], w2s, start=True, stop=False)
                    mm(BY[0:NB, 64:64 + KC], ones[0:1, 0:NB], rows[0:1, CH:CH + KC], start=False, stop=True).then_inc(att_mm, 1)
                if g == 3:
                    pe.wait_ge(sel_in, 16)
                    pe.wait_ge(att_done, 1)
                    for t in range(NT):
                        v = mm(BT[:, 64 + KC * t:64 + KC * (t + 1)], sel[:, t], att[:], start=True, stop=True)
                    v.then_inc(attx_mm, 1)
            pe.wait_ge(pg_done, OCT)
            pe.wait_ge(pu_done, OCT)

            def hidden(n, half):
                c = n % HC
                if n < 2:
                    pe.wait_ge(convt_done, NT - 1 + n)
                if n % HC == 0:
                    pe.wait_ge(y0hi_done, (half + 1) * TPH)
                    pe.wait_ge(y0lo_done, (half + 1) * TPH)
                for banks, tab, used, made in ((G, mg, silu_done, g_mm), (UU, mu, h_done, u_mm)):
                    if n >= 2:
                        pe.wait_ge(used, n - 1)
                    for r in range(R):
                        for part, y in enumerate((y0hi, y0lo)):
                            v = mm(banks[n % 2][:], tab[:, r, c], y[:, r, HALF * half:HALF * (half + 1)],
                                   start=(r == 0 and part == 0), stop=(r == R - 1 and part == 1))
                    v.then_inc(made, 1)

            def y(j):
                pe.wait_ge(acc_done, j + 1)
                if j >= 1:
                    pe.wait_ge(y_done, j)
                mm(BY[:], bd[:, j], acc[:, j], start=True, stop=True).then_inc(y_mm, 1)

            def yt(j):
                pe.wait_ge(y_done, j + 1)
                if j >= 1:
                    pe.wait_ge(yt_done, j)
                for c in range(DC):
                    v = nc.tensor.transpose(BT[:, P * c:P * (c + 1)], yv[:, j % 2, P * c:P * (c + 1)], ident)
                v.then_inc(yt_mm, 1)

            def logits(j):
                pe.wait_ge(yt_done, j + 1)
                if j >= 1:
                    pe.wait_ge(amat_done, j)
                if j == TPH - 1:
                    pe.wait_ge(slots_done, j)
                for c in range(DC):
                    v = mm(logit_bank(j)[:, 0:E], yT[:, c], gwt[:, c], start=(c == 0), stop=(c == DC - 1))
                v.then_inc(lg_mm, 1)

            def positions(j):
                pe.wait_ge(amat_done, j + 1)
                if j >= 1:
                    pe.wait_ge(slots_done, j)
                for t in range(j):
                    mm(position_bank(j)[:, E:2 * E], cbf[:, B_ONE:B_ONE + P], amat[:, t], start=(t == 0), stop=False)
                mm(position_bank(j)[:, E:2 * E], cbf[:, B_UP:B_UP + P], amat[:, j], start=(j == 0), stop=True).then_inc(pos_mm, 1)

            def bias(j):
                if j >= TPH:
                    pe.wait_ge(acc2_done, j - TPH + 1)
                mm(EBB[j % TPH][:], combT[:, j], eb[:], start=True, stop=True).then_inc(eb_mm, 1)

            L = TPH - 1
            beside_hidden = {0: (y, L), 1: (positions, L - 1), 2: (yt, L), 4: (logits, L), 7: (positions, L)}

            def beside_down(j):
                t = j % TPH
                return {**({1: (y, j - 1), 4: (yt, j - 1), 8: (logits, j - 1)} if t >= 1 else {}),
                        **({6: (positions, j - 2)} if t >= 2 else {})}

            def weights_across(half):
                pe.wait_ge(choice_done, (half + 1) * TPH)
                if half == 1:
                    pe.wait_ge(y_done, NT)
                for t in range(TPH):
                    v = nc.tensor.transpose((G[1], BY)[half][0:E, P * t:P * (t + 1)], comb[:, TPH * half + t], ident)
                v.then_inc(combt_mm, 1)

            def down(j):
                half, t = divmod(j, TPH)
                if j >= 2:
                    pe.wait_ge(acc_done, j - 1)
                if j == TPH:
                    pe.wait_ge(slots_done, TPH)
                steps = beside_down(j)
                if j == NT - 1:
                    steps[HC - 2] = (weights_across, 0)
                for c in range(HC):
                    if t == 0:
                        pe.wait_ge(hhi_done, half * HC + c + 1)
                        pe.wait_ge(hlo_done, half * HC + c + 1)
                    for part, h in enumerate((hhi, hlo)):
                        v = mm(DN[j % 2][:], h[:, c, P * t:P * (t + 1)], md[:, c], start=(c == 0 and part == 0), stop=(c == HC - 1 and part == 1))
                    if c == HC - 1:
                        v.then_inc(d_mm, 1)
                    if c in steps:
                        step, tile = steps[c]
                        step(tile)

            for half in range(2):
                for c in range(HC):
                    if half == 1 and c == 1:
                        pe.wait_ge(amat_done, TPH - 1)
                    hidden(half * HC + c, half)
                    if half == 0 and c < OCT:
                        if c == 0:
                            pe.wait_ge(attx_done, 1)
                            pe.wait_ge(tern_done, 3)
                        table(c, 2, PD, pd_mm, pd_done)
                    if half == 1 and c in beside_hidden:
                        step, tile = beside_hidden[c]
                        step(tile)
                pe.wait_ge(pd_done, OCT)
                for t in range(TPH):
                    down(half * TPH + t)
            y(NT - 1)
            pe.wait_ge(eb_in, 16)
            pe.wait_ge(combt_done, 1)
            bias(0)
            yt(NT - 1)
            positions(NT - 2)
            logits(NT - 1)
            bias(1)
            positions(NT - 1)
            weights_across(1)
            for j in range(2, TPH):
                bias(j)
            pe.wait_ge(combt_done, 2)
            for j in range(TPH, NT):
                bias(j)

            def transposes(t, n, b, first=False):
                pe.wait_ge(yg_in[b], n * 16)
                if not first:
                    pe.wait_ge(xt_done, t - 1)
                for c in range(DC):
                    v = nc.tensor.transpose(XT[b % 2][:, P * c:P * (c + 1)], yg[b][:, P * c:P * (c + 1)], ident)
                v.then_inc(xt_mm, 1)

            def product(t, n, b, u, first=False):
                pe.wait_ge(xt_done, t + 1)
                pe.wait_ge(w_in[u], n * 64)
                if not first:
                    pe.wait_ge(res_done, t - 1)
                for c in range(DC):
                    v = mm(RS[u % 2][:], xT[u % 2][:, c], wbuf[:, bass.ds(b, 1), c].rearrange("p a d -> p (a d)"), start=(c == 0), stop=(c == DC - 1))
                v.then_inc(r_mm, 1)

            transposes(0, 1, 0, True)
            pe.wait_ge(acc2_done, NT)
            for j in range(NT):
                v = mm(BY[0:E, 0:1], amat[:, j], cbf[:, B_ONE:B_ONE + 1], start=(j == 0), stop=(j == NT - 1))
            v.then_inc(cnt_mm, 1)
            transposes(1, 1, 1, True)
            product(0, 1, 0, 0, True)
            pe.wait_ge(more_done, 1)
            mm(BY[0:E, 0:1], cf[0:E, C_TRI:C_TRI + E], more[:], start=True, stop=True).then_inc(incl_mm, 1)
            pe.wait_ge(before_done, 1)
            mm(BY[0:1, 0:XMAX], ones[0:E, 0:1], before[:], start=True, stop=True)
            mm(BY[0:1, XMAX:2 * XMAX], more[:], before[:], start=True, stop=True)
            mm(BY[0:1, 2 * XMAX:2 * XMAX + 1], more[:], ones[0:E, 0:1], start=True, stop=True).then_inc(list_mm, 1)
            for t in range(2, U):
                transposes(t, 1, t)
                product(t - 1, 1, t - 1, t - 1, t - 1 < 2)
            transposes(U, 2, 0)
            product(U - 1, 1, U - 1, U - 1)
            with pe.Fori(1, G0) as g:
                for u in range(U):
                    if u < U - 1:
                        transposes(g * U + (u + 1), g + 1, u + 1)
                    else:
                        transposes(g * U + U, g + 2, 0)
                    product(g * U + u, g + 1, g % 2 * U + u, u)
            for u in range(XU):
                if u < XU - 1:
                    transposes(E + u + 1, G0 + 1, u + 1)
                product(E + u, G0 + 1, u, u)
            pe.wait_ge(todo_done, 1)
            bodies = pe.value_load(todo[0:1, 2 * XMAX:2 * XMAX + 1], min_val=0, max_val=XMAX // XU - 1)
            with pe.If(bodies > 0):
                with pe.Fori(1, bodies + 1) as g:
                    for u in range(XU):
                        transposes(g * XU + (E + u), g + (G0 + 1), u)
                    for u in range(XU):
                        product(g * XU + (E + u), g + (G0 + 1), u, u)


def layouts(i):
    import numpy as np

    f = np.float32
    x = i["x"]
    out = {}
    xp = np.zeros((R, CH, NB, QW), f)
    xp[:, :, :, 1:1 + P] = x.reshape(NB, CH, P, R).transpose(3, 1, 0, 2)
    out["xp"] = xp.reshape(P, NB, QW)
    out["x"] = x.reshape(TOK, D)
    cw = i["L0_cond_weight"]
    per = CH // 4
    wc = np.zeros((R, CH, 3, R, CH), f)
    for s in range(R):
        for d in range(3):
            for r in range(R):
                tap = 4 * (d - 1) + s - r + 4
                if 0 <= tap < TAPS:
                    for co in range(CH):
                        g0 = co // per * per
                        wc[s, g0:g0 + per, d, r, co] = cw[co, :, tap]
    out["wc"] = wc.reshape(P, 3, P)

    def hidden_pad(w, axis):
        shape = list(w.shape)
        shape[axis] = HC * OB
        p = np.zeros(shape, f)
        p[tuple(slice(0, n) for n in w.shape)] = w
        return p

    base = np.zeros((P, 3, BW), f)
    for m, k in enumerate(("L0_ffn_w_gate", "L0_ffn_w_up")):
        w = hidden_pad(i[k], 1).reshape(OCT, HC * OB, OB, R)
        base[:, m] = w.transpose(0, 2, 3, 1).reshape(P, BW)
    w = hidden_pad(i["L0_ffn_w_down"], 2).reshape(OCT, OUT8, HC, OB)
    base[:, 2] = w.transpose(0, 3, 2, 1).reshape(P, BW)
    out["base"] = base
    o = {"cond": i["cond_128"].T, "cwt": i["L0_cond_c_weight"].T}
    o["rows"] = np.zeros((P, CH + KC), f)
    o["rows"][0] = np.concatenate([i["fside_S_0"], i["L1_cond_b2"]])
    o["b01"] = np.stack([i["L1_cond_b0"], i["L1_cond_b1"]], 1)
    o["w0"], o["w1"], o["w2"] = i["L1_cond_W0"], i["L1_cond_W1"], i["L1_cond_W2"]
    o["wrep"] = np.tile(i["L1_cond_weight"][..., 0].transpose(2, 1, 0), (NPT, 1, 1))
    o["bkr"] = np.tile(i["L1_cond_bias_k"].T, (NPT, 1))
    o["gwt"] = i["L1_ffn_gate_w"].T.reshape(DC, P, E).transpose(1, 0, 2)
    out["w"] = i["L1_ffn_expert_w"].reshape(E, D, DC, P).transpose(0, 3, 2, 1)
    out["eb"] = i["L1_ffn_expert_b"]

    def bf16_bits(v):
        return (np.ascontiguousarray(v).view(np.uint32) >> 16).astype(np.uint16).reshape(P, -1).view(f)

    sel = np.zeros((NB, NT, P), f)
    for b in range(NB):
        sel[b, b // NPT, b % NPT * CH:(b % NPT + 1) * CH] = 1
    out["sel"] = sel
    S = np.zeros((OCT, OCT, OCT), f)
    S[0, 0, 0] = 1
    for n in range(1, OCT):
        S[0, n, n] = S[n, 0, n] = 1
        S[n, n, 0] = -1
    for t in ((1, 2, 3), (1, 4, 5), (1, 7, 6), (2, 4, 6), (2, 5, 7), (3, 4, 7), (3, 6, 5)):
        for v in range(3):
            p_, q_, r_ = t[v], t[(v + 1) % 3], t[(v + 2) % 3]
            S[p_, q_, r_], S[q_, p_, r_] = 1, -1
    perm = np.zeros((OCT, OB, OCT, OCT, OB), f)
    for j in range(OCT):
        for n in range(OCT):
            for k in range(OCT):
                for d in range(OB):
                    perm[j, d, k, n, d] = S[j, n, k]
    o["perm"] = bf16_bits(perm.reshape(P, OCT, P))
    cf = np.zeros((P, CF_W), f)
    cf[:, C_ID:C_ID + P] = np.eye(P)
    cf[:, C_IO:C_IO + E] = np.arange(E)
    cf[:, C_MK:C_MK + NPT] = np.arange(P)[:, None] // CH == np.arange(NPT)
    cf[0:E, C_TRI:C_TRI + E] = np.triu(np.ones((E, E)))
    cf[:, C_THR:C_THR + 8] = np.append(np.arange(1, CHUNKS) * P, 2 * TOK)
    cf[:, C_ONE:C_ONE + P] = 1
    out["cf"] = cf
    cb = np.ones((P, CB_W), f)
    cb[:, B_UP:B_UP + P] = np.triu(np.ones((P, P)), 1)
    o["cbf"] = bf16_bits(cb)
    rec = np.zeros((P, NT, 2, 4), np.int32)
    tok = np.arange(TOK).reshape(NT, P).T
    rec[:, :, :, 0] = tok[:, :, None]
    rec[:, :, :, 1] = tok[:, :, None]
    o["rec"] = rec.view(f)
    for group, parts in GROUPS.items():
        out[group] = np.concatenate([np.ascontiguousarray(o[n]).reshape(P, w) for n, w in parts], 1)
    pads = np.zeros((P, E, 4), np.int32)
    pads[:, :, 0] = PADROW
    pads[:, :, 1] = TOK + np.arange(P)[:, None]
    out["pads"] = pads.reshape(P, E * 4)
    return {k: np.ascontiguousarray(v) for k, v in out.items()}


def kernel(**inputs):
    import numpy as np
    import concourse.bacc as bacc
    from concourse.bass_utils import run_bass_kernel_spmd

    arrays = layouts({k: np.asarray(v) for k, v in inputs.items()})
    nc = bacc.Bacc("TRN2", target_bir_lowering=False, num_devices=1)
    a = {k: nc.dram_tensor(f"in_{k}", v.shape, mybir.dt.from_np(v.dtype), kind="ExternalInput").ap() for k, v in arrays.items()}
    a["out"] = nc.dram_tensor("out", (TOK + P, D), F32, kind="ExternalOutput").ap()
    build_adaln_ffn(nc, a)
    r = run_bass_kernel_spmd(nc, [{f"in_{k}": v for k, v in arrays.items()}], core_ids=[0])
    return r.results[0]["out"][0:TOK].reshape(NB, CH, D)
```
